# Optimizing a Trainium2 kernel written in Bass

```python
import numpy as np
import jax
import jax.numpy as jnp

def _softmax(x, axis=-1):
    return jax.nn.softmax(x, axis=axis)

def _gelu(x):
    return jax.nn.gelu(x, approximate=True)

def _silu(x):
    return jax.nn.silu(x)

def _sigmoid(x):
    return jax.nn.sigmoid(x)

def _layernorm(x, axis=-1, eps=1e-05):
    m = jnp.mean(x, axis=axis, keepdims=True)
    v = jnp.var(x, axis=axis, keepdims=True)
    return (x - m) / jnp.sqrt(v + eps)

def _scatter_add(tgt, idx, src, axis=0):
    return tgt.at[idx].add(src)

def _segment_sum(src, seg, n):
    return jax.ops.segment_sum(src, seg, n)
kernel_name = 'mk_seq_postln_d1_jaxref_r4_750f96'

def setup_inputs(seed: int=0):
    np.random.seed(seed)
    _w = jnp.asarray

    def _L0_attn_setup():
        import jax, jax.numpy as jnp
        import numpy as np
        from jax import lax
        H = 256
        EXPAND = 2
        I = EXPAND * H
        N = 16
        K = 4
        R = 64
        EPS = 1e-06
        B_SZ, L = (2, 256)

        def rmsnorm(x, w):
            v = jnp.mean(x.astype(jnp.float32) ** 2, axis=-1, keepdims=True)
            return w * (x * jax.lax.rsqrt(v + EPS)).astype(x.dtype)
        key = jax.random.key(seed)
        ks = jax.random.split(key, 10)
        s = 0.02
        inp = {'hidden_states': jax.random.normal(ks[0], (B_SZ, L, H), jnp.float32), 'in_proj_w': jax.random.normal(ks[1], (2 * I, H), jnp.float32) * s, 'conv_w': jax.random.normal(ks[2], (I, 1, K), jnp.float32) * s, 'conv_b': jnp.zeros((I,), jnp.float32), 'x_proj_w': jax.random.normal(ks[3], (R + 2 * N, I), jnp.float32) * s, 'dt_proj_w': jax.random.normal(ks[4], (I, R), jnp.float32) * s, 'dt_proj_b': jax.random.normal(ks[5], (I,), jnp.float32) * 0.1, 'dt_ln_w': jnp.ones((R,), jnp.float32), 'b_ln_w': jnp.ones((N,), jnp.float32), 'c_ln_w': jnp.ones((N,), jnp.float32), 'A_log': jnp.log(jnp.broadcast_to(jnp.arange(1, N + 1, dtype=jnp.float32)[None, :], (I, N))), 'D': jnp.ones((I,), jnp.float32), 'out_proj_w': jax.random.normal(ks[6], (H, I), jnp.float32) * s}
        return inp
    _L0_attn_in = _L0_attn_setup()

    def _L0_ffn_setup():
        import jax, jax.numpy as jnp
        import numpy as np
        B, S, D_MODEL, D_FF = (4, 512, 256, 1024)

        def _quantum_transform(hidden, theta, w_real, w_imag):
            imag = w_imag * jnp.sin(theta + hidden * 0.1)
            quantum_phase = jnp.cos(theta) * w_real + jnp.sin(theta) * w_imag
            return hidden + quantum_phase * imag * 0.1
        key = jax.random.key(seed)
        ks = jax.random.split(key, 8)
        return {'x': jax.random.normal(ks[0], (B, S, D_MODEL), dtype=jnp.float32), 'W1': jax.random.normal(ks[1], (D_MODEL, D_FF), dtype=jnp.float32) * (1.0 / np.sqrt(D_MODEL)), 'b1': jnp.zeros((D_FF,), dtype=jnp.float32), 'quantum_phases': jax.random.normal(ks[2], (D_FF,), dtype=jnp.float32) * (2.0 * np.pi), 'quantum_weights_real': jax.random.normal(ks[3], (D_FF,), dtype=jnp.float32) * 0.1, 'quantum_weights_imag': jax.random.normal(ks[4], (D_FF,), dtype=jnp.float32) * 0.1, 'W2': jax.random.normal(ks[5], (D_FF, D_MODEL), dtype=jnp.float32) * (1.0 / np.sqrt(D_FF)), 'b2': jnp.zeros((D_MODEL,), dtype=jnp.float32)}
    _L0_ffn_in = _L0_ffn_setup()
    _d = {'L0_attn_hidden_states': _L0_attn_in['hidden_states'], 'L0_attn_in_proj_w': _L0_attn_in['in_proj_w'], 'L0_attn_conv_w': _L0_attn_in['conv_w'], 'L0_attn_conv_b': _L0_attn_in['conv_b'], 'L0_attn_x_proj_w': _L0_attn_in['x_proj_w'], 'L0_attn_dt_proj_w': _L0_attn_in['dt_proj_w'], 'L0_attn_dt_proj_b': _L0_attn_in['dt_proj_b'], 'L0_attn_dt_ln_w': _L0_attn_in['dt_ln_w'], 'L0_attn_b_ln_w': _L0_attn_in['b_ln_w'], 'L0_attn_c_ln_w': _L0_attn_in['c_ln_w'], 'L0_attn_A_log': _L0_attn_in['A_log'], 'L0_attn_D': _L0_attn_in['D'], 'L0_attn_out_proj_w': _L0_attn_in['out_proj_w'], 'L0_ffn_W1': _L0_ffn_in['W1'], 'L0_ffn_b1': _L0_ffn_in['b1'], 'L0_ffn_quantum_phases': _L0_ffn_in['quantum_phases'], 'L0_ffn_quantum_weights_real': _L0_ffn_in['quantum_weights_real'], 'L0_ffn_quantum_weights_imag': _L0_ffn_in['quantum_weights_imag'], 'L0_ffn_W2': _L0_ffn_in['W2'], 'L0_ffn_b2': _L0_ffn_in['b2']}
    _x0 = _d['L0_attn_hidden_states']
    _d['L0_attn_hidden_states'] = jax.random.normal(jax.random.fold_in(jax.random.key(seed), 1), (8, 1024, 256), dtype=_x0.dtype)
    del _x0
    return _d

def reference(L0_attn_hidden_states, L0_attn_in_proj_w, L0_attn_conv_w, L0_attn_conv_b, L0_attn_x_proj_w, L0_attn_dt_proj_w, L0_attn_dt_proj_b, L0_attn_dt_ln_w, L0_attn_b_ln_w, L0_attn_c_ln_w, L0_attn_A_log, L0_attn_D, L0_attn_out_proj_w, L0_ffn_W1, L0_ffn_b1, L0_ffn_quantum_phases, L0_ffn_quantum_weights_real, L0_ffn_quantum_weights_imag, L0_ffn_W2, L0_ffn_b2):

    def _L0_attn_ref(hidden_states, in_proj_w, conv_w, conv_b, x_proj_w, dt_proj_w, dt_proj_b, dt_ln_w, b_ln_w, c_ln_w, A_log, D, out_proj_w):
        import jax, jax.numpy as jnp
        import numpy as np
        from jax import lax
        H = 256
        EXPAND = 2
        I = EXPAND * H
        N = 16
        K = 4
        R = 64
        EPS = 1e-06
        B_SZ, L = (2, 256)

        def rmsnorm(x, w):
            v = jnp.mean(x.astype(jnp.float32) ** 2, axis=-1, keepdims=True)
            return w * (x * jax.lax.rsqrt(v + EPS)).astype(x.dtype)
        b, l, _ = hidden_states.shape
        proj = hidden_states @ in_proj_w.T
        hs, gate = (proj[..., :I], proj[..., I:])
        x = jnp.transpose(hs, (0, 2, 1))
        x = lax.conv_general_dilated(x, conv_w, (1,), [(1, 2)], feature_group_count=I, dimension_numbers=('NCH', 'OIH', 'NCH'))
        x = x + conv_b[None, :, None]
        u = jax.nn.silu(jnp.transpose(x, (0, 2, 1)))
        x_dbl = u @ x_proj_w.T
        dt = rmsnorm(x_dbl[..., :R], dt_ln_w)
        Bm = rmsnorm(x_dbl[..., R:R + N], b_ln_w)
        Cm = rmsnorm(x_dbl[..., R + N:], c_ln_w)
        dt = jax.nn.softplus(dt @ dt_proj_w.T + dt_proj_b)
        A = -jnp.exp(A_log)
        dA = jnp.exp(dt[..., None] * A)
        dBu = (dt * u)[..., None] * Bm[:, :, None, :]

        def step(h, inp):
            dA_t, dBu_t = inp
            h = dA_t * h + dBu_t
            return (h, h)
        h0 = jnp.zeros((b, I, N), jnp.float32)
        _, h_seq = lax.scan(step, h0, (jnp.transpose(dA, (1, 0, 2, 3)), jnp.transpose(dBu, (1, 0, 2, 3))))
        y = jnp.einsum('lbin,bln->bli', h_seq, Cm)
        y = y + u * D
        y = y * jax.nn.silu(gate)
        return y @ out_proj_w.T

    def _L0_ffn_ref(x, W1, b1, quantum_phases, quantum_weights_real, quantum_weights_imag, W2, b2):
        import jax, jax.numpy as jnp
        import numpy as np
        B, S, D_MODEL, D_FF = (4, 512, 256, 1024)

        def _quantum_transform(hidden, theta, w_real, w_imag):
            imag = w_imag * jnp.sin(theta + hidden * 0.1)
            quantum_phase = jnp.cos(theta) * w_real + jnp.sin(theta) * w_imag
            return hidden + quantum_phase * imag * 0.1
        hidden = jnp.einsum('bsd,df->bsf', x, W1) + b1
        q = _quantum_transform(hidden, quantum_phases, quantum_weights_real, quantum_weights_imag)
        act = jax.nn.relu(q)
        return jnp.einsum('bsf,fd->bsd', act, W2) + b2
    x = L0_attn_hidden_states
    x = _layernorm(x + _L0_attn_ref(x, L0_attn_in_proj_w, L0_attn_conv_w, L0_attn_conv_b, L0_attn_x_proj_w, L0_attn_dt_proj_w, L0_attn_dt_proj_b, L0_attn_dt_ln_w, L0_attn_b_ln_w, L0_attn_c_ln_w, L0_attn_A_log, L0_attn_D, L0_attn_out_proj_w), axis=-1)
    x = _layernorm(x + _L0_ffn_ref(x, L0_ffn_W1, L0_ffn_b1, L0_ffn_quantum_phases, L0_ffn_quantum_weights_real, L0_ffn_quantum_weights_imag, L0_ffn_W2, L0_ffn_b2), axis=-1)
    return x

_drawn_inputs = setup_inputs


def setup_inputs(seed=0):
    import zlib

    import numpy as np

    out = dict(_drawn_inputs(seed))
    spreads = {'L0_attn_conv_b': (0.0, 0.8),
     'L0_attn_dt_ln_w': (1.0, 0.6),
     'L0_attn_b_ln_w': (1.0, 0.6),
     'L0_attn_c_ln_w': (1.0, 0.6),
     'L0_attn_D': (1.0, 0.6),
     'L0_ffn_b1': (0.0, 0.1),
     'L0_ffn_b2': (0.0, 0.1)}
    factors = {'L0_attn_in_proj_w': 8.0,
     'L0_attn_conv_w': 8.0,
     'L0_attn_x_proj_w': 4.032,
     'L0_attn_dt_proj_w': 8.0,
     'L0_attn_dt_proj_b': 8.0,
     'L0_attn_A_log': 8.0,
     'L0_attn_out_proj_w': 8.0,
     'L0_ffn_quantum_phases': 8.0,
     'L0_ffn_quantum_weights_real': 35.658,
     'L0_ffn_quantum_weights_imag': 8.0}
    for name, (base, spread) in spreads.items():
        noise = np.random.default_rng([zlib.crc32(name.encode()), seed]).standard_normal(out[name].shape)
        drawn = base * np.exp(spread * noise) if base else spread * noise
        out[name] = jnp.asarray(drawn.astype(out[name].dtype))
    for name, factor in factors.items():
        out[name] = (out[name] * factor).astype(out[name].dtype)
    return out
```

```python
import concourse.bass as bass
from concourse import mybir
from contextlib import ExitStack

B, L, H = 8, 1024, 256
I, N, R, K = 512, 16, 64, 4
F = 1024
P = 128
TS = P // B
TILES = L // TS
MI, MH, MF = I // P, H // P, F // P
RING = 4
AHEAD, BEHIND = 4, 4
HSTEPS = 8
XW = R + 2 * N

PCOLS = {"conv_w": MI * K, "conv_b": MI, "A_log": MI * N, "D": MI, "b1": MF, "theta": MF, "w_re": MF,
         "w_im": MF, "bw": 1, "cw": 1, "dtw": 1}
POFF, _o = {}, 0
for _k, _n in PCOLS.items():
    POFF[_k] = (_o, _o + _n)
    _o += _n
PTOTAL = _o

ROUND = 12582912.0
TWO_PI = 6.283185307179586
INV_2PI = 1.0 / TWO_PI
PI_A = 6.28125
PI_B = 0.0019350051879882812
PI_C = TWO_PI - PI_A - PI_B
SIN_SCALE = 6.283185
EXP_LN_SET = 6
EPS_RMS, EPS_LN = 1e-6, 1e-5
SPLITS, CONVS = 5, 3
SP_CAP = 80.0


class Tiles:

    def __init__(self, reg, static):
        self.reg, self.static = reg, static

    def on(self, k):
        return self.reg is not None or 0 <= self.static + k < TILES

    def slot(self, k, n):
        return (self.static + k) % n

    def count(self, k, per=1, plus=0):
        c = per * (self.static + k + 1) + plus
        return max(c, 0) if self.reg is None else self.reg * (RING * per) + c

    def uses(self, k, n):
        c = (self.static + k) // n + 1
        return max(c, 0) if self.reg is None else self.reg * (RING // n) + c

    def tile(self, k):
        c = self.static + k
        return c if self.reg is None else self.reg * RING + c


def min_tile(j, k, per):
    if j.reg is None and j.static + k >= TILES:
        return per * TILES
    return j.count(k, per)


def iterations(eng, body):
    for j in range(-AHEAD, BEHIND):
        body(Tiles(None, j))
    with eng.Fori(0, (TILES - AHEAD - BEHIND) // RING) as it:
        for q in range(RING):
            body(Tiles(it, BEHIND + q))
    for j in range(TILES - AHEAD, TILES + BEHIND):
        body(Tiles(None, j))


def mamba_ffn_kernel(nc, x, w_in, w_x, w_dt, w_out, w1, w2, params, b2, consts, out):
    f32, bf16 = mybir.dt.float32, mybir.dt.bfloat16
    ALU, ACT, AX = mybir.AluOpType, mybir.ActivationFunctionType, mybir.AxisListType
    MUL, ADD, SUB, MAX, MIN = ALU.mult, ALU.add, ALU.subtract, ALU.max, ALU.min
    V, G, S, T = nc.vector, nc.gpsimd, nc.scalar, nc.tensor

    x_t = x.rearrange("b (n h g) c -> n h g b c", h=4, g=4)
    out_t = out.rearrange("b (n h g) c -> n h g b c", h=4, g=4)

    ctx = ExitStack()
    with ctx:
        def sb(name, shape, dt=f32):
            return ctx.enter_context(nc.sbuf_tensor(name, shape, dt))

        def bank(name):
            return ctx.enter_context(nc.psum_tensor(name, [P, 512], f32))

        def sem(name):
            return ctx.enter_context(nc.semaphore(name))

        win = sb("win", [P, MH, 2 * I])
        wx = sb("wx", [P, MI, XW])
        wdt = sb("wdt", [R + 1, I])
        wo = sb("wo", [P, MI, H])
        wf1 = sb("wf1", [P, MH, F])
        wf2 = sb("wf2", [P, MF, H])
        prm = sb("prm", [P, PTOTAL])
        b2_bc = sb("b2_bc", [P, H])
        cst = sb("cst", [P, 4 * P + TS])
        ident, mask = cst[:, 0:P], cst[:, P:2 * P]
        unperm = cst[:, 3 * P:4 * P]
        steps_of = cst[:, 4 * P:4 * P + TS]
        identb = sb("identb", [P, P], bf16)
        sel = sb("sel", [P, P], bf16)
        eps_rms = sb("eps_rms", [P, 1])
        eps_ln = sb("eps_ln", [P, 1])
        one = sb("one", [P, 1])
        Aneg = sb("Aneg", [P, MI * N])
        turn0 = sb("turn0", [P, MF])
        amp = sb("amp", [P, MF])
        tt = sb("tt", [P, 8, MF])

        xn = sb("xn", [P, 2, H])
        xk = sb("xk", [P, RING, H])
        xT = sb("xT", [P, MH, P])
        xkT = sb("xkT", [P, MH, P])
        RT = RING * P
        hs = sb("hs", [P, MI, B + RT + 2 * B])
        cv = sb("cv", [P, K, MI, P])
        u = sb("u", [P, RING, MI, P])
        xd2 = sb("xd2", [P, XW])
        ms = sb("ms", [P, 8])
        rs = sb("rs", [P, 4])
        dtn = sb("dtn", [P, R])
        lb = sb("lb", [P, P])
        lc = sb("lc", [P, P])
        dtT = sb("dtT", [R + 1, P])
        bs = sb("bs", [P, RING, TS])
        CZ = 4 * 32 + B
        cz = sb("cz", [P, RING, 4, CZ])
        sp = sb("sp", [P, MI, P])
        dts = sb("dts", [P, 2, MI, P])
        xf = sb("xf", [P, 2, MI, P])
        xs = sb("xs", [P, MI, TS, 4, B], bf16)
        xsT = sb("xsT", [P, 2, 4, I], bf16)
        a1 = sb("a1", [P, 2, MI, TS, P])
        ah = sb("ah", [P, I])
        hst = sb("hst", [P, HSTEPS, I])
        ysb = sb("ysb", [P, I])
        sg = sb("sg", [P, 2, MI, P])
        vg = sb("vg", [P, MI, P])
        r1 = sb("r1", [P, H])
        st1 = sb("st1", [P, 12])
        x1 = sb("x1", [P, H])
        x1b = sb("x1b", [P, RING, H])
        x1T = sb("x1T", [P, MH, P])
        hid = sb("hid", [P, 2, MF, P])
        zt = sb("zt", [P, MF, P])
        kf = sb("kf", [P, MF, P])
        r2 = sb("r2", [P, H])
        st2 = sb("st2", [P, 12])
        ot = sb("ot", [P, 2, H])

        aT = [bank("aT0"), bank("aT1")]
        xb = [bank("xb0"), bank("xb1")]
        yacc = bank("yacc")
        G0, G1, G2 = bank("G0"), bank("G1"), bank("G2")
        xsP = G0[:, :].bitcast(bf16)

        m_in = sem("weights_loaded")
        m_xn = [sem("xn_loaded0"), sem("xn_loaded1")]
        m_xk = [sem(f"xk_loaded{i}") for i in range(RING)]
        m_out = [sem("out_stored0"), sem("out_stored1")]
        s_set = {e: sem(f"setup_{e}") for e in ("dve", "act", "pool")}
        s_aT, s_xb = sem("aT_ready"), sem("xb_ready")
        s_ah, s_h = sem("ah_ready"), sem("h_ready")
        s_c = sem("c_products")
        s_exp, s_yev, s_yT, s_v, s_yg = map(sem, ("exp_ready", "y_copied", "yT_ready", "v_ready", "yg_ready"))
        s_xT, s_xTe, s_xkT, s_xkTe = map(sem, ("xT_ready", "xT_copied", "xkT_ready", "xkT_copied"))
        s_hs, s_hse = sem("hs_ready"), sem("hs_copied")
        s_cc, s_u = sem("conv_steps"), sem("u_ready")
        s_gate, s_sg = sem("gate_ready"), sem("silu_gate_ready")
        s_xd, s_sq, s_red, s_ra, s_rs, s_l = map(sem, ("xd_ready", "xd_squared", "xd_reduced", "rms_ln", "rms_ready", "norms_applied"))
        s_rc = sem("reduce_chain")
        s_fs, s_fse, s_dtp, s_e1, s_sp, s_dt = map(sem, ("small_ready", "small_copied", "dtp_ready", "dt_exp", "softplus_ready", "dt_ready"))
        s_xm = sem("split_steps")
        s_xsT, s_xse = sem("xsT_ready"), sem("xsT_copied")
        s_o, s_r1, s_b1, s_n1a, s_n1, s_x1, s_x1b = map(sem, ("out_proj_ready", "r1_ready", "ln1_stats", "ln1_ln", "ln1_rstd", "x1_ready", "x1b_ready"))
        s_q1 = sem("ln1_chain")
        s_x1T, s_x1Te = sem("x1T_ready"), sem("x1T_copied")
        s_hm, s_hid = sem("hidden_ready"), sem("hidden_copied")
        s_z, s_k, s_f, s_sin, s_cs, s_q, s_act = map(sem, ("turns_ready", "turns_rounded", "turns_reduced", "sine_ready", "sine_scaled", "q_ready", "act_ready"))
        s_w2, s_r2, s_b2, s_n2a, s_n2, s_ln2 = map(sem, ("ffn_ready", "r2_ready", "ln2_stats", "ln2_ln", "ln2_rstd", "ln2_ready"))
        s_q2 = sem("ln2_chain")
        s_passed = sem("passed")

        def prow(name, rows=P):
            a, b = POFF[name]
            return prm[0:rows, a:b]

        N_LOADS = 9
        DVE_SETUP = 29

        block = ctx.enter_context(nc.Block())

        @block.sync
        def _(sp_):
            for dst, src in ((win[:, :, :], w_in), (cst[:, :], consts), (prm[:, :], params), (wx[:, :, :], w_x),
                             (wdt[:, :], w_dt), (wo[:, :, :], w_out), (wf1[:, :, :], w1), (wf2[:, :, :], w2),
                             (b2_bc[:, :], b2)):
                sp_.dma_start(dst, src).then_inc(m_in, 16)
            for slot in range(2):
                sp_.sem_inc(m_out[slot], 1)

            def body(j):
                if j.on(4):
                    sp_.wait_ge(s_xT, j.count(2))
                    slot = j.slot(4, 2)
                    for i in range(4):
                        sp_.dma_start(xn[32 * i:32 * (i + 1), slot, :], x_t[bass.ds(j.tile(4), 1), i, :, :, :]
                                      .rearrange("n h b c -> (n h) b c")).then_inc(m_xn[slot], 16)
                if j.on(0):
                    sp_.wait_ge(s_r1, j.count(-RING))
                    slot = j.slot(0, RING)
                    for g in range(4):
                        sp_.dma_start(xk[32 * g:32 * (g + 1), slot, :], x_t[bass.ds(j.tile(0), 1), g, :, :, :]
                                      .rearrange("n h b c -> (n h) b c")).then_inc(m_xk[slot], 16)
                if j.on(-4):
                    sp_.wait_ge(s_ln2, j.count(-4))
                    slot = j.slot(-4, 2)
                    for g in range(4):
                        sp_.dma_start(out_t[bass.ds(j.tile(-4), 1), g, :, :, :].rearrange("n h b c -> (n h) b c"),
                                      ot[32 * g:32 * (g + 1), slot, :]).then_inc(m_out[slot], 16)
            iterations(sp_, body)
            for slot in range(2):
                sp_.wait_ge(m_out[slot], 16 * 4 * TILES // 2 + 1)

        @block.tensor
        def _(pe):
            pe.wait_ge(m_in, 16 * N_LOADS)
            pe.wait_ge(s_set["dve"], DVE_SETUP)

            def scan_operands(j, t):
                if t == 0:
                    pe.wait_ge(s_exp, j.count(0))
                pe.wait_ge(s_ah, j.count(-1, TS, t - 1))
                for k in range(MI):
                    last = T.transpose(aT[t % 2][:, P * k:P * (k + 1)], a1[:, j.slot(0, 2), k, t, :], ident)
                last.then_inc(s_aT, 1)
                if t == 0:
                    pe.wait_ge(s_xse, j.count(0, 2))
                pe.wait_ge(s_h, j.count(-1, TS, t - 1))
                g, h = t % 4, t // 4
                rows = slice(32 * g, 32 * g + 24)
                T.matmul(xb[t % 2][:, :], sel[rows, :], xsT[rows, j.slot(0, 2), h, :],
                         start=True, stop=True).then_inc(s_xb, 1)

            def c_products(j, k, h):
                pe.wait_ge(s_h, j.count(k - 1, TS, 4 * h + 4))
                if h == 0:
                    pe.wait_ge(s_yev, j.count(k - 1))
                columns = cz[:, j.slot(k, RING), :, :].rearrange("p h c -> p (h c)")
                for g in range(4):
                    t = 4 * h + g
                    last = T.matmul(yacc[32 * g:32 * g + 32, :], columns[:, 32 * t:32 * (t + 1)], hst[:, t % HSTEPS, :],
                                    start=(h == 0), stop=(h == 3))
                last.then_inc(s_c, 1)

            def up(outp, w, col0, m0, m1, rhs):
                for m in range(m0, m1):
                    for k in range(MH):
                        last = T.matmul(outp[:, P * (m - m0):P * (m - m0 + 1)],
                                        w[:, k, col0 + P * m:col0 + P * (m + 1)], rhs[:, k, :],
                                        start=(k == 0), stop=(k == MH - 1))
                return last

            def ffn_down(j, k, blocks):
                for b in blocks:
                    last = T.matmul(G0[:, 0:H], kf[:, b, :], wf2[:, b, :], start=(b == 0), stop=(b == MF - 1))
                if blocks[-1] == MF - 1:
                    last.then_inc(s_w2, 1)

            def out_proj(j, blocks):
                for m in blocks:
                    last = T.matmul(G2[:, 0:H], vg[:, m, :], wo[:, m, :], start=(m == 0), stop=(m == MI - 1))
                if blocks[-1] == MI - 1:
                    last.then_inc(s_o, 1)

            def body(j):
                for t in range(TS):
                    if j.on(0):
                        scan_operands(j, t)
                    if t == 0 and j.on(-3):
                        up(G1[:, 2 * P:4 * P], wf1, 0, 6, 8, x1T).then_inc(s_hm, 1)
                    if t == 0 and j.on(-4):
                        ffn_down(j, -4, (1, 2))
                    if t == 1 and j.on(-4):
                        ffn_down(j, -4, (3, 4))
                    if t == 1 and j.on(-1):
                        c_products(j, -1, 3)
                    if t == 2 and j.on(-4):
                        ffn_down(j, -4, (5, 6, 7))
                    if t == 2 and (j.on(-1) or j.on(4)):
                        pe.wait_ge(s_hid, min_tile(j, -3, 2))
                        pe.wait_ge(s_dt, min_tile(j, 1, 1))
                        if j.on(-1):
                            slot = j.slot(-1, RING)
                            pe.wait_ge(m_xk[slot], j.uses(-1, RING) * (16 * 4))
                            for k in range(MH):
                                last = T.transpose(G1[:, P * k:P * (k + 1)], xk[:, slot, P * k:P * (k + 1)], ident)
                            last.then_inc(s_xkT, 1)
                        if j.on(4):
                            slot = j.slot(4, 2)
                            pe.wait_ge(m_xn[slot], j.uses(4, 2) * (16 * 4))
                            for k in range(MH):
                                last = T.transpose(G1[:, H + P * k:H + P * (k + 1)], xn[:, slot, P * k:P * (k + 1)], ident)
                            last.then_inc(s_xT, 1)
                    if t in (3, 6) and j.on(-2):
                        pe.wait_ge(s_yg, j.count(-2))
                        out_proj(j, (0, 1) if t == 3 else (2, 3))
                    if t in (4, 5) and j.on(-1):
                        if t == 4:
                            pe.wait_ge(s_xkTe, j.count(-1))
                            pe.wait_ge(s_r2, j.count(-4))
                            pe.wait_ge(s_xse, min_tile(j, 0, 2))
                        m = 2 * (t - 4)
                        last = up(G0[:, P * m:P * (m + 2)], win, I, m, m + 2, xkT)
                        if t == 5:
                            last.then_inc(s_gate, 1)
                    if t == 7 and j.on(2):
                        pe.wait_ge(s_u, j.count(2))
                        pe.wait_ge(s_xTe, min_tile(j, 4, 1))
                        pe.wait_ge(s_xkTe, j.count(-1))
                        for m in range(MI):
                            last = T.matmul(G1[:, 0:XW], u[:, j.slot(2, RING), m, :], wx[:, m, :],
                                            start=(m == 0), stop=(m == MI - 1))
                        last.then_inc(s_xd, 1)
                    if t == 7 and j.on(0):
                        c_products(j, 0, 0)
                    if t in (8, 9) and j.on(4):
                        if t == 8:
                            pe.wait_ge(s_xTe, j.count(4))
                            pe.wait_ge(s_sg, j.count(-1))
                            pe.wait_ge(s_hse, j.count(3))
                            pe.wait_ge(s_xse, j.count(0, 2))
                        m = 2 * (t - 8)
                        last = up(G0[:, P * m:P * (m + 2)], win, 0, m, m + 2, xT)
                        if t == 9:
                            last.then_inc(s_hs, 1)
                    if t == 10 and j.on(2):
                        pe.wait_ge(s_l, j.count(2))
                        T.transpose(G1[:, 256:384], lc[:, :], ident)
                        T.transpose(G1[0:R, 128:256], dtn[:, :], ident)
                        T.matmul(G1[:, 384:384 + TS], lb[:, :], steps_of, start=True, stop=True).then_inc(s_fs, 1)
                    if t == 10 and j.on(0):
                        c_products(j, 0, 1)
                    if t == 10 and j.on(-2):
                        pe.wait_ge(s_x1, j.count(-2))
                        for k in range(MH):
                            last = T.transpose(G2[:, P * k:P * (k + 1)], x1[:, P * k:P * (k + 1)], ident)
                        last.then_inc(s_x1T, 1)
                    if t in (11, 13) and j.on(1):
                        part = (t - 11) // 2
                        if part == 0:
                            pe.wait_ge(s_xm, j.count(1, SPLITS))
                            pe.wait_ge(s_hse, min_tile(j, 4, 1))
                            pe.wait_ge(s_sg, j.count(-1))
                        else:
                            pe.wait_ge(s_xse, j.count(0, 2, 1))
                        for h in (2 * part, 2 * part + 1):
                            for m in range(MI):
                                c = I * (h - 2 * part) + P * m
                                last = T.transpose(xsP[:, c:c + P],
                                                   xs[:, m, 4 * h:4 * h + 4, :, :].rearrange("p g a b -> p (g a b)"), identb[:, :])
                        last.then_inc(s_xsT, 1)
                    if t == 12 and j.on(2):
                        pe.wait_ge(s_fse, j.count(2))
                        for m in range(MI):
                            last = T.matmul(G1[:, P * m:P * (m + 1)], wdt[:, P * m:P * (m + 1)], dtT[:, :],
                                            start=True, stop=True)
                        last.then_inc(s_dtp, 1)
                    if t in (12, 13) and j.on(-2):
                        pe.wait_ge(s_x1Te, j.count(-2))
                        m = 2 * (t - 12)
                        last = up(G2[:, P * m:P * (m + 2)], wf1, 0, m, m + 2, x1T)
                        if t == 13:
                            last.then_inc(s_hm, 1)
                    if t == 14 and j.on(0):
                        c_products(j, 0, 2)
                    if t == 15 and j.on(-3):
                        pe.wait_ge(s_act, j.count(-3))
                        pe.wait_ge(s_xse, min_tile(j, 1, 2))
                        pe.wait_ge(s_sg, min_tile(j, -1, 1))
                        ffn_down(j, -3, (0,))
                    if t == 15 and j.on(-2):
                        pe.wait_ge(s_dt, min_tile(j, 2, 1))
                        pe.wait_ge(s_xkTe, min_tile(j, -1, 1))
                        up(G1[:, 0:2 * P], wf1, 0, 4, 6, x1T)
                    if t == 15 and j.on(-1):
                        pe.wait_ge(s_yev, j.count(-1))
                        pe.wait_ge(s_hid, j.count(-2, 2, -1))
                        for m in range(MI):
                            last = T.transpose(G2[:, P * m:P * (m + 1)], ysb[:, P * m:P * (m + 1)], unperm)
                        last.then_inc(s_yT, 1)
            iterations(pe, body)

        @block.scalar
        def _(act):
            act.wait_ge(m_in, 16 * N_LOADS)
            act.wait_ge(s_set["dve"], DVE_SETUP - 5)

            def exp_ln_tables():
                S.add_instruction(mybir.InstLoadActFuncSet(name=nc.get_next_instruction_name(), act_func_set_id=EXP_LN_SET,
                                                           engine=mybir.EngineType.Activation))

            S.activation(tt[:, 3, :], tt[:, 1, :], ACT.Sin, scale=SIN_SCALE).then_inc(s_set["act"], 1)
            S.activation(tt[:, 4, :], tt[:, 2, :], ACT.Sin, scale=SIN_SCALE).then_inc(s_set["act"], 1)
            S.activation(Aneg[:, :], prow("A_log"), ACT.Exp).then_inc(s_set["act"], 1)
            exp_ln_tables()
            act.wait_ge(s_set["dve"], DVE_SETUP)

            def flat(ap):
                return ap.rearrange("p a b -> p (a b)")

            def exponentials(j, e0, e1):
                if e0 == 0:
                    act.wait_ge(s_dt, j.count(1))
                    act.wait_ge(s_aT, j.count(-1, TS))
                for e in range(e0, e1):
                    m, n = divmod(e, N)
                    o = a1[:, j.slot(1, 2), m, :, n:P:N]
                    i = dts[:, j.slot(1, 2), m, :].rearrange("p (t b) -> p t b", b=B)
                    last = S.activation(o, i, ACT.Exp, scale=Aneg[:, e:e + 1])
                if e1 == MI * N:
                    last.then_inc(s_exp, 1)

            def rstd(src, dst, eps, s_half, s_done, need):
                S.activation(dst, src, ACT.Ln, bias=eps).then_inc(s_half, 1)
                act.wait_ge(s_half, need)
                S.activation(dst, dst, ACT.Exp, scale=-0.5).then_inc(s_done, 1)

            def body(j):
                for t in range(TS):
                    if j.on(1):
                        exponentials(j, 4 * t, 4 * t + 4)
                    if t == 1 and j.on(-3):
                        hidden_copy(j, -3, 1)
                    if t == 2 and j.on(-1):
                        act.wait_ge(s_c, j.count(-1, 4))
                        act.wait_ge(s_yT, j.count(-2))
                        S.copy(ysb[:, :], yacc[:, :]).then_inc(s_yev, 1)
                    if t == 3 and (j.on(-1) or j.on(4)):
                        act.wait_ge(s_xT, min_tile(j, 4, 1))
                        act.wait_ge(s_xkT, j.count(-1))
                    if t == 3 and j.on(-1):
                        act.wait_ge(s_gate, j.count(-2))
                        S.copy(flat(xkT[:, :, :]), G1[:, 0:H]).then_inc(s_xkTe, 1)
                    if t == 3 and j.on(4):
                        act.wait_ge(s_hs, j.count(3))
                        S.copy(flat(xT[:, :, :]), G1[:, H:2 * H]).then_inc(s_xTe, 1)
                    if t == 6 and j.on(-1):
                        act.wait_ge(s_gate, j.count(-1))
                        act.wait_ge(s_yg, j.count(-3))
                        S.activation(flat(sg[:, j.slot(-1, 2), :, :]), G0[:, :], ACT.Silu).then_inc(s_sg, 1)
                    if t == 6 and j.on(2):
                        act.wait_ge(s_cc, j.count(2, CONVS))
                        act.wait_ge(s_v, j.count(-2))
                        S.activation(u[:, j.slot(2, RING), :, :], cv[:, 0, :, :], ACT.Silu).then_inc(s_u, 1)
                    if t == 6 and j.on(-3):
                        act.wait_ge(s_f, j.count(-3))
                        S.activation(kf[:, :, :], kf[:, :, :], ACT.Sin, scale=SIN_SCALE).then_inc(s_sin, 1)
                    if t == 6:
                        exp_ln_tables()
                    if t == 5 and j.on(-4):
                        act.wait_ge(s_b2, j.count(-4))
                        rstd(st2[:, 7:8], st2[:, 8:9], eps_ln[:, :], s_n2a, s_n2, j.count(-4))
                    if t == 8 and j.on(2):
                        act.wait_ge(s_xd, j.count(2))
                        act.wait_ge(s_red, j.count(1))
                        S.activation(xd2[:, :], G1[:, 0:XW], ACT.Square).then_inc(s_sq, 1)
                    if t == 8 and j.on(-2):
                        act.wait_ge(s_b1, j.count(-2))
                        rstd(st1[:, 7:8], st1[:, 8:9], eps_ln[:, :], s_n1a, s_n1, j.count(-2))
                    if t == 8 and j.on(2):
                        act.wait_ge(s_red, j.count(2))
                        rstd(ms[:, 4:7], rs[:, 0:3], eps_rms[:, :], s_ra, s_rs, j.count(2))
                    if t == 10 and j.on(4):
                        hs_copy(j)
                    if t == 11 and j.on(-2):
                        act.wait_ge(s_x1T, j.count(-2))
                        act.wait_ge(s_hm, j.count(-3, 2))
                        S.copy(flat(x1T[:, :, :]), G2[:, 0:H]).then_inc(s_x1Te, 1)
                    if t == 13 and j.on(2):
                        act.wait_ge(s_dtp, j.count(2))
                        act.wait_ge(s_dt, j.count(1))
                        S.activation(flat(sp[:, :, :]), G1[:, :], ACT.Exp).then_inc(s_e1, 1)
                        act.wait_ge(s_e1, j.count(2))
                        S.activation(flat(sp[:, :, :]), flat(sp[:, :, :]), ACT.Ln, bias=one[:, :]).then_inc(s_sp, 1)
                    if t in (12, 14) and j.on(1):
                        part = (t - 12) // 2
                        act.wait_ge(s_xsT, j.count(0, 2, part + 1))
                        act.wait_ge(s_xb, j.count(-1, TS))
                        S.copy(flat(xsT[:, j.slot(1, 2), 2 * part:2 * part + 2, :]), xsP).then_inc(s_xse, 1)
                    if t == 14 and j.on(-3):
                        act.wait_ge(s_q, j.count(-3))
                        S.activation(kf[:, :, :], kf[:, :, :], ACT.Relu).then_inc(s_act, 1)
                    if t == 14 and j.on(-2):
                        hidden_copy(j, -2, 0)

            def hidden_copy(j, k, half):
                act.wait_ge(s_hm, j.count(k - 1, 2, half + 1))
                if half == 0:
                    act.wait_ge(s_q, j.count(k - 2))
                for m in range(4):
                    last = S.activation(hid[:, j.slot(k, 2), 4 * half + m, :], (G2, G1)[half][:, P * m:P * (m + 1)],
                                        ACT.Identity, bias=prow("b1")[:, 4 * half + m:4 * half + m + 1])
                last.then_inc(s_hid, 1)

            def hs_copy(j):
                act.wait_ge(s_hs, j.count(4))
                act.wait_ge(s_cc, j.count(1, CONVS))
                slot = j.slot(4, RING)
                src = G0[:, :].rearrange("p (m t) -> p m t", m=MI)
                last = S.copy(hs[:, :, B + P * slot:B + P * (slot + 1)], src)
                if slot == RING - 1:
                    last = S.copy(hs[:, :, 0:B], src[:, :, P - B:P])
                if slot == 0:
                    last = S.copy(hs[:, :, B + RT:B + RT + 2 * B], src[:, :, 0:2 * B])
                last.then_inc(s_hse, 1)

            iterations(act, body)

        @block.vector
        def _(dve):
            dve.wait_ge(m_in, 16 * N_LOADS)
            done = [0]

            def setup(ins):
                ins.then_inc(s_set["dve"], 1)
                done[0] += 1
                dve.wait_ge(s_set["dve"], done[0])

            th, inv = prow("theta"), INV_2PI
            setup(V.tensor_scalar(tt[:, 0, :], th, inv, ROUND, MUL, ADD))
            setup(V.tensor_scalar(tt[:, 0, :], tt[:, 0, :], ROUND, None, SUB))
            setup(V.scalar_tensor_tensor(tt[:, 5, :], tt[:, 0, :], -PI_A, th, MUL, ADD))
            setup(V.scalar_tensor_tensor(tt[:, 5, :], tt[:, 0, :], -PI_B, tt[:, 5, :], MUL, ADD))
            setup(V.scalar_tensor_tensor(tt[:, 5, :], tt[:, 0, :], -PI_C, tt[:, 5, :], MUL, ADD))
            setup(V.tensor_scalar(turn0[:, :], tt[:, 5, :], inv, None, MUL))
            setup(V.tensor_scalar(tt[:, 1, :], turn0[:, :], 0.5, -0.5, MIN, MAX))
            setup(V.tensor_scalar(tt[:, 6, :], turn0[:, :], 0.25, None, ADD))
            setup(V.tensor_scalar(tt[:, 7, :], tt[:, 6, :], ROUND, ROUND, ADD, SUB))
            setup(V.tensor_tensor(tt[:, 2, :], tt[:, 6, :], tt[:, 7, :], SUB))
            setup(V.memset(eps_rms[:, :], EPS_RMS))
            setup(V.memset(eps_ln[:, :], EPS_LN))
            setup(V.memset(one[:, :], 1.0))
            setup(V.tensor_copy(identb[:, :], ident))
            setup(V.tensor_copy(sel[:, :], cst[:, 2 * P:3 * P]))
            setup(V.tensor_scalar(wx[:, :, 0:R], wx[:, :, 0:R], R ** -0.5, None, MUL))
            setup(V.tensor_scalar(wx[:, :, R:XW], wx[:, :, R:XW], N ** -0.5, None, MUL))
            setup(V.tensor_scalar(prow("bw"), prow("bw"), N ** 0.5, None, MUL))
            setup(V.tensor_scalar(prow("cw"), prow("cw"), N ** 0.5, None, MUL))
            setup(V.tensor_scalar(wdt[0:R, :], wdt[0:R, :], prow("dtw", R), R ** 0.5, MUL, MUL))
            setup(V.memset(dtT[R:R + 1, :], 1.0))
            setup(V.memset(cz[:, :, :, :], 0.0))
            setup(V.memset(xs[:, :, :, :, :], 0.0))
            setup(V.memset(hst[:, HSTEPS - 1, :], 0.0))
            dve.wait_ge(s_set["act"], 3)
            setup(V.tensor_scalar(Aneg[:, :], Aneg[:, :], -1.0, None, MUL))
            setup(V.tensor_tensor(tt[:, 4, :], tt[:, 4, :], prow("w_re"), MUL))
            setup(V.tensor_tensor(tt[:, 3, :], tt[:, 3, :], prow("w_im"), MUL))
            setup(V.tensor_tensor(tt[:, 4, :], tt[:, 4, :], tt[:, 3, :], ADD))
            setup(V.scalar_tensor_tensor(amp[:, :], tt[:, 4, :], 0.1, prow("w_im"), MUL, MUL))
            assert done[0] == DVE_SETUP

            def scan_step(j, t):
                dve.wait_ge(s_aT, j.count(-1, TS, t + 1))
                dve.wait_ge(s_h, j.count(-1, TS, t))
                V.tensor_tensor(ah[:, :], aT[t % 2][:, :], hst[:, (t - 1) % HSTEPS, :], MUL).then_inc(s_ah, 1)
                dve.wait_ge(s_xb, j.count(-1, TS, t + 1))
                dve.wait_ge(s_ah, j.count(-1, TS, t + 1))
                if t % 4 == 0:
                    dve.wait_ge(s_c, j.count(-1, 4, t // 4 - 1))
                V.scalar_tensor_tensor(hst[:, t % HSTEPS, :], xb[t % 2][:, :], bs[:, j.slot(0, RING), t:t + 1], ah[:, :],
                                       MUL, ADD).then_inc(s_h, 1)

            def norm_stats(r, st, s_chain, s_done, need):
                V.bn_stats(st[:, 0:6], r).then_inc(s_chain, 1)
                dve.wait_ge(s_chain, need)
                dve.sem_inc(s_passed, 1)
                V.bn_aggr(st[:, 6:8], st[:, 0:6]).then_inc(s_done, 1)

            def body(j):
                for t in range(TS):
                    if j.on(0):
                        scan_step(j, t)
                    if t == 3 and j.on(-4):
                        dve.wait_ge(s_w2, j.count(-4))
                        dve.wait_ge(s_x1b, j.count(-4))
                        V.tensor_tensor(r2[:, :], G0[:, 0:H], x1b[:, j.slot(-4, RING), :], ADD).then_inc(s_r2, 1)
                        dve.wait_ge(s_r2, j.count(-4))
                        norm_stats(r2[:, :], st2, s_q2, s_b2, j.count(-4))
                    if t == 1 and j.on(-2):
                        dve.wait_ge(s_yT, j.count(-2))
                        dve.wait_ge(s_o, j.count(-3))
                        for m in range(MI):
                            last = V.scalar_tensor_tensor(vg[:, m, :], u[:, j.slot(-2, RING), m, :], prow("D")[:, m:m + 1],
                                                          G2[:, P * m:P * (m + 1)], MUL, ADD)
                        last.then_inc(s_v, 1)
                    if t == 4 and j.on(-3):
                        dve.wait_ge(s_z, j.count(-3, 2))
                        dve.wait_ge(s_w2, j.count(-4))
                        V.tensor_scalar(kf[:, :, :], zt[:, :, :], ROUND, ROUND, ADD, SUB).then_inc(s_k, 1)
                    if t == 8 and j.on(-4):
                        dve.wait_ge(s_n2, j.count(-4))
                        slot = j.slot(-4, 2)
                        dve.wait_ge(m_out[slot], (j.uses(-4, 2) - 1) * (16 * 4) + 1)
                        V.tensor_scalar(ot[:, slot, :], r2[:, :], st2[:, 6:7], st2[:, 8:9], SUB, MUL).then_inc(s_ln2, 1)
                    if t == 7 and j.on(-2):
                        dve.wait_ge(s_o, j.count(-2))
                        dve.wait_ge(s_x1, j.count(-3))
                        V.tensor_tensor(r1[:, :], G2[:, 0:H], xk[:, j.slot(-2, RING), :], ADD).then_inc(s_r1, 1)
                        dve.wait_ge(s_r1, j.count(-2))
                        norm_stats(r1[:, :], st1, s_q1, s_b1, j.count(-2))
                    if t == 8 and j.on(2):
                        dve.wait_ge(s_sq, j.count(2))
                        dve.wait_ge(s_rs, j.count(1))
                        V.tensor_reduce(ms[:, 0:6], xd2[:, :].rearrange("p (a b) -> p a b", b=N), AX.X, ADD).then_inc(s_rc, 1)
                        dve.wait_ge(s_rc, j.count(2))
                        V.tensor_reduce(ms[:, 6:7], ms[:, 0:4], AX.X, ADD).then_inc(s_red, 1)
                    if t == 9 and j.on(2):
                        dve.wait_ge(s_rs, j.count(2))
                        dve.wait_ge(s_fs, j.count(1))
                        V.tensor_scalar(dtn[:, :], G1[:, 0:R], rs[:, 2:3], None, MUL)
                        for dst, c0, r in ((lb, R, 0), (lc, R + N, 1)):
                            v3 = lambda ap: ap.rearrange("p (b n) -> p b n", n=N)
                            src = G1[:, c0:c0 + N].rearrange("p (a n) -> p a n", a=1).to_broadcast([P, B, N])
                            last = V.scalar_tensor_tensor(v3(dst[:, :]), src, rs[:, r:r + 1], v3(mask), MUL, MUL)
                        last.then_inc(s_l, 1)
                    if t == 10 and j.on(-4):
                        dve.wait_ge(s_ln2, j.count(-4))
                    if t == 9 and j.on(-2):
                        dve.wait_ge(s_n1, j.count(-2))
                        dve.wait_ge(s_x1T, j.count(-3))
                        dve.wait_ge(s_x1b, j.count(-3))
                        V.tensor_scalar(x1[:, :], r1[:, :], st1[:, 6:7], st1[:, 8:9], SUB, MUL).then_inc(s_x1, 1)
                    if t == 11 and j.on(2):
                        dve.wait_ge(s_fs, j.count(2))
                        dve.wait_ge(s_dtp, j.count(1))
                        slot = j.slot(2, RING)
                        V.tensor_copy(dtT[0:R, :], G1[0:R, 128:256])
                        V.tensor_scalar(bs[:, slot, :], G1[:, 384:384 + TS], prow("bw"), None, MUL)
                        dve.wait_ge(s_c, j.count(-2, 4))
                        V.tensor_scalar(cz[:, slot, :, 0:P].rearrange("p h (g c) -> p h g c", g=4)[:, :, :, 0:B],
                                        G1[:, 256:384].rearrange("p (h g b) -> p h g b", h=4, g=4),
                                        prow("cw"), None, MUL).then_inc(s_fse, 1)
                    flat = sp[:, :, :].rearrange("p a b -> p (a b)")
                    if t == 14 and j.on(2):
                        dve.wait_ge(s_sp, j.count(2))
                        dve.wait_ge(s_exp, j.count(0))
                        dve.wait_ge(s_xm, j.count(0, SPLITS))
                        V.scalar_tensor_tensor(dts[:, j.slot(2, 2), :, :].rearrange("p a b -> p (a b)"), G1[:, :], SP_CAP, flat,
                                               MAX, MIN).then_inc(s_dt, 1)
            iterations(dve, body)

        @block.gpsimd
        def _(pool):
            pool.wait_ge(m_in, 16 * N_LOADS)
            pool.wait_ge(s_set["dve"], DVE_SETUP)
            G.memset(hs[:, :, 0:B], 0.0).then_inc(s_set["pool"], 1)
            pool.wait_ge(s_set["pool"], 1)

            def alone():
                pool.sem_inc(s_passed, 1)

            def turns(j, k, half):
                pool.wait_ge(s_hid, j.count(k - 1, 2, half + 1))
                if half == 0:
                    pool.wait_ge(s_f, j.count(k - 1))
                alone()
                for m in range(4 * half, 4 * half + 4):
                    last = G.tensor_scalar(zt[:, m, :], hid[:, j.slot(k, 2), m, :], 0.1 * INV_2PI, turn0[:, m:m + 1], MUL, ADD)
                last.then_inc(s_z, 1)

            def body(j):
                flat = lambda ap: ap.rearrange("p a b -> p (a b)")
                if j.on(-2):
                    pool.wait_ge(s_v, j.count(-2))
                    pool.wait_ge(s_sg, j.count(-2))
                    G.tensor_tensor(flat(vg[:, :, :]), flat(vg[:, :, :]), flat(sg[:, j.slot(-2, 2), :, :]), MUL).then_inc(s_yg, 1)
                if j.on(-3):
                    turns(j, -3, 1)
                    pool.wait_ge(s_z, j.count(-3, 2))
                    pool.wait_ge(s_k, j.count(-3))
                    G.tensor_tensor(flat(kf[:, :, :]), flat(zt[:, :, :]), flat(kf[:, :, :]), SUB).then_inc(s_f, 1)
                if j.on(1):
                    pool.wait_ge(s_dt, j.count(1))
                    pool.wait_ge(s_u, j.count(1))
                    pool.wait_ge(s_xsT, j.count(0, 2))
                    base = lambda i: j.count(0, SPLITS, i)
                    part = lambda a: xs[:, :, :, a, :].rearrange("p m t b -> p (m t) b")
                    v = lambda ap: ap.rearrange("p m (t b) -> p (m t) b", b=B)
                    x0, x1_ = xf[:, 0, :, :], xf[:, 1, :, :]
                    G.tensor_tensor(flat(x0), flat(dts[:, j.slot(1, 2), :, :]), flat(u[:, j.slot(1, RING), :, :]), MUL).then_inc(s_xm, 1)
                    pool.wait_ge(s_xm, base(1))
                    alone()
                    G.tensor_scalar(part(0), v(x0), 1.0, 1.0, MUL, MUL).then_inc(s_xm, 1)
                    pool.wait_ge(s_xm, base(2))
                    G.tensor_tensor(v(x1_), v(x0), part(0), SUB).then_inc(s_xm, 1)
                    pool.wait_ge(s_xm, base(3))
                    alone()
                    G.tensor_scalar(part(1), v(x1_), 1.0, 1.0, MUL, MUL).then_inc(s_xm, 1)
                    pool.wait_ge(s_xm, base(4))
                    G.tensor_tensor(part(2), v(x1_), part(1), SUB).then_inc(s_xm, 1)
                if j.on(-3):
                    pool.wait_ge(s_sin, j.count(-3))
                    alone()
                    for m in range(MF):
                        last = G.tensor_scalar(kf[:, m, :], kf[:, m, :], amp[:, m:m + 1], 1.0, MUL, MUL)
                    last.then_inc(s_cs, 1)
                    pool.wait_ge(s_cs, j.count(-3))
                    G.tensor_tensor(flat(kf[:, :, :]), flat(kf[:, :, :]), flat(hid[:, j.slot(-3, 2), :, :]), ADD).then_inc(s_q, 1)
                if j.on(-2):
                    pool.wait_ge(s_x1, j.count(-2))
                    G.tensor_tensor(x1b[:, j.slot(-2, RING), :], x1[:, :], b2_bc[:, :], ADD).then_inc(s_x1b, 1)
                if j.on(3):
                    if j.on(4):
                        pool.wait_ge(s_hse, j.count(4))
                    else:
                        pool.wait_ge(s_hse, j.count(3))
                        G.memset(hs[:, :, B + RT:B + RT + 2 * B], 0.0).then_inc(s_set["pool"], 1)
                        pool.wait_ge(s_set["pool"], 2)
                    pool.wait_ge(s_u, j.count(2))
                    alone()
                    base = lambda i: j.count(2, CONVS, i)
                    c0 = P * j.slot(3, RING)
                    for k in range(K):
                        for m in range(MI):
                            src = hs[:, m, c0 + B * k:c0 + B * k + P]
                            w = prow("conv_w")[:, K * m + k:K * m + k + 1]
                            if k == 0:
                                last = G.tensor_scalar(cv[:, k, m, :], src, w, prow("conv_b")[:, m:m + 1], MUL, ADD)
                            else:
                                last = G.tensor_scalar(cv[:, k, m, :], src, w, 1.0, MUL, MUL)
                    last.then_inc(s_cc, 1)
                    pool.wait_ge(s_cc, base(1))
                    G.tensor_tensor(flat(cv[:, 0, :, :]), flat(cv[:, 0, :, :]), flat(cv[:, 1, :, :]), ADD)
                    G.tensor_tensor(flat(cv[:, 2, :, :]), flat(cv[:, 2, :, :]), flat(cv[:, 3, :, :]), ADD).then_inc(s_cc, 1)
                    pool.wait_ge(s_cc, base(2))
                    G.tensor_tensor(flat(cv[:, 0, :, :]), flat(cv[:, 0, :, :]), flat(cv[:, 2, :, :]), ADD).then_inc(s_cc, 1)
                if j.on(-2):
                    turns(j, -2, 0)
            iterations(pool, body)


def kernel(**inputs):
    import numpy as np
    import concourse.bacc as bacc
    from concourse.bass_utils import run_bass_kernel_spmd

    a = {k[3:]: np.asarray(v) for k, v in inputs.items()}

    def cols(v, n):
        return np.ascontiguousarray(np.moveaxis(v.reshape(n, P, -1), 0, 1)).reshape(P, -1)

    rows = {"conv_w": cols(a["attn_conv_w"], MI), "conv_b": cols(a["attn_conv_b"], MI), "A_log": cols(a["attn_A_log"], MI),
            "D": cols(a["attn_D"], MI), "b1": cols(a["ffn_b1"], MF), "theta": cols(a["ffn_quantum_phases"], MF),
            "w_re": cols(a["ffn_quantum_weights_real"], MF), "w_im": cols(a["ffn_quantum_weights_imag"], MF),
            "bw": np.tile(a["attn_b_ln_w"], B)[:, None], "cw": np.tile(a["attn_c_ln_w"], B)[:, None],
            "dtw": np.tile(a["attn_dt_ln_w"], P // R)[:, None]}
    params = np.concatenate([rows[k] for k in PCOLS], axis=1)

    p = np.arange(P)
    ident = np.eye(P, dtype=np.float32)
    mask = (p[:, None] % B == p[None, :] // N).astype(np.float32)
    sel = mask * (p[:, None] % 32 < 24)
    unperm = (p[:, None] // 32 + 4 * (p[:, None] % 32 // B) == p[None, :] // B) * (p[:, None] % B == p[None, :] % B)
    steps = p[:, None] // B == np.arange(TS)[None, :]
    consts = np.concatenate([ident, mask, sel, unperm, steps], axis=1).astype(np.float32)

    def blocks(v, n):
        return np.ascontiguousarray(v.reshape(n, P, -1).transpose(1, 0, 2))

    arrays = {
        "x": a["attn_hidden_states"],
        "w_in": blocks(a["attn_in_proj_w"].T, MH), "w_x": blocks(a["attn_x_proj_w"].T, MI),
        "w_dt": np.concatenate([a["attn_dt_proj_w"].T, a["attn_dt_proj_b"][None, :]], axis=0),
        "w_out": blocks(a["attn_out_proj_w"].T, MI), "w1": blocks(a["ffn_W1"], MH), "w2": blocks(a["ffn_W2"], MF),
        "params": params, "b2": np.ascontiguousarray(np.broadcast_to(a["ffn_b2"], (P, H))), "consts": consts,
    }
    nc = bacc.Bacc("TRN2", target_bir_lowering=False, num_devices=1, dynamic_dma_scratch_size=1024)
    feeds, args = {}, []
    for name, v in arrays.items():
        v = np.ascontiguousarray(v)
        feeds[f"in_{name}"] = v
        args.append(nc.dram_tensor(f"in_{name}", v.shape, mybir.dt.from_np(v.dtype), kind="ExternalInput").ap())
    args.append(nc.dram_tensor("out_0", (B, L, H), mybir.dt.float32, kind="ExternalOutput").ap())
    mamba_ffn_kernel(nc, *args)
    r = run_bass_kernel_spmd(nc, [feeds], core_ids=[0])
    return r.results[0]["out_0"]
```

```python
import concourse.bass as bass
from concourse import mybir
from contextlib import ExitStack

B, L, H = 8, 1024, 256
I, N, R, K = 512, 16, 64, 4
F = 1024
P = 128
TS = P // B
TILES = L // TS
MI, MH, MF = I // P, H // P, F // P
RING = 4
AHEAD, BEHIND = 4, 4
HSTEPS = 8
XW = R + 2 * N

PCOLS = {"conv_w": MI * K, "conv_b": MI, "A_log": MI * N, "D": MI, "b1": MF, "theta": MF, "w_re": MF,
         "w_im": MF, "bw": 1, "cw": 1, "dtw": 1}
POFF, _o = {}, 0
for _k, _n in PCOLS.items():
    POFF[_k] = (_o, _o + _n)
    _o += _n
PTOTAL = _o

ROUND = 12582912.0
TWO_PI = 6.283185307179586
INV_2PI = 1.0 / TWO_PI
PI_A = 6.28125
PI_B = 0.0019350051879882812
PI_C = TWO_PI - PI_A - PI_B
SIN_SCALE = 6.283185
EXP_LN_SET = 6
EPS_RMS, EPS_LN = 1e-6, 1e-5
EXPS = (0, 6, 10, 15, 21, 23, 23, 26, 31, 37, 43, 48, 53, 57, 61, 64, 64)
WHOLE = (1, 2, 4, 7, 8, 10, 13, 14)
SPLITS, CONVS = 5, 3
SP_CAP = 80.0


class Tiles:

    def __init__(self, reg, static):
        self.reg, self.static = reg, static

    def on(self, k):
        return self.reg is not None or 0 <= self.static + k < TILES

    def slot(self, k, n):
        return (self.static + k) % n

    def count(self, k, per=1, plus=0):
        c = per * (self.static + k + 1) + plus
        return max(c, 0) if self.reg is None else self.reg * (RING * per) + c

    def uses(self, k, n):
        c = (self.static + k) // n + 1
        return max(c, 0) if self.reg is None else self.reg * (RING // n) + c

    def tile(self, k):
        c = self.static + k
        return c if self.reg is None else self.reg * RING + c


def min_tile(j, k, per):
    if j.reg is None and j.static + k >= TILES:
        return per * TILES
    return j.count(k, per)


def iterations(eng, body):
    for j in range(-AHEAD, BEHIND):
        body(Tiles(None, j))
    with eng.Fori(0, (TILES - AHEAD - BEHIND) // RING) as it:
        for q in range(RING):
            body(Tiles(it, BEHIND + q))
    for j in range(TILES - AHEAD, TILES + BEHIND):
        body(Tiles(None, j))


def mamba_ffn_kernel(nc, x, w_in, w_x, w_dt, w_out, w1, w2, params, b2, consts, out):
    f32, bf16 = mybir.dt.float32, mybir.dt.bfloat16
    ALU, ACT, AX = mybir.AluOpType, mybir.ActivationFunctionType, mybir.AxisListType
    MUL, ADD, SUB, MAX, MIN = ALU.mult, ALU.add, ALU.subtract, ALU.max, ALU.min
    V, G, S, T = nc.vector, nc.gpsimd, nc.scalar, nc.tensor

    x_t = x.rearrange("b (n h g) c -> n h g b c", h=4, g=4)
    out_t = out.rearrange("b (n h g) c -> n h g b c", h=4, g=4)

    ctx = ExitStack()
    with ctx:
        def sb(name, shape, dt=f32):
            return ctx.enter_context(nc.sbuf_tensor(name, shape, dt))

        def bank(name):
            return ctx.enter_context(nc.psum_tensor(name, [P, 512], f32))

        def sem(name):
            return ctx.enter_context(nc.semaphore(name))

        win = sb("win", [P, MH, 2 * I])
        wx = sb("wx", [P, MI, XW])
        wdt = sb("wdt", [R + 1, I])
        wo = sb("wo", [P, MI, H])
        wf1 = sb("wf1", [P, MH, F])
        wf2 = sb("wf2", [P, MF, H])
        prm = sb("prm", [P, PTOTAL])
        b2_bc = sb("b2_bc", [P, H])
        cst = sb("cst", [P, 4 * P + TS])
        ident, mask = cst[:, 0:P], cst[:, P:2 * P]
        unperm = cst[:, 3 * P:4 * P]
        steps_of = cst[:, 4 * P:4 * P + TS]
        identb = sb("identb", [P, P], bf16)
        sel = sb("sel", [P, P], bf16)
        eps_rms = sb("eps_rms", [P, 1])
        eps_ln = sb("eps_ln", [P, 1])
        one = sb("one", [P, 1])
        Aneg = sb("Aneg", [P, MI * N])
        turn0 = sb("turn0", [P, MF])
        amp = sb("amp", [P, MF])
        tt = sb("tt", [P, 8, MF])

        xn = sb("xn", [P, 2, H])
        xk = sb("xk", [P, RING, H])
        xT = sb("xT", [P, MH, P])
        xkT = sb("xkT", [P, MH, P])
        RT = RING * P
        hs = sb("hs", [P, MI, B + RT + 2 * B])
        cv = sb("cv", [P, K, MI, P])
        u = sb("u", [P, RING, MI, P])
        xd2 = sb("xd2", [P, XW])
        ms = sb("ms", [P, 8])
        rs = sb("rs", [P, 4])
        dtn = sb("dtn", [P, R])
        lb = sb("lb", [P, P])
        lc = sb("lc", [P, P])
        dtT = sb("dtT", [R + 1, P])
        bs = sb("bs", [P, RING, TS])
        CZ = 4 * 32 + B
        cz = sb("cz", [P, RING, 4, CZ])
        sp = sb("sp", [P, MI, P])
        dts = sb("dts", [P, 2, MI, P])
        xf = sb("xf", [P, 2, MI, P])
        xs = sb("xs", [P, MI, TS, 4, B], bf16)
        xsT = sb("xsT", [P, 2, 4, I], bf16)
        a1 = sb("a1", [P, 2, MI, TS, P])
        ah = sb("ah", [P, I])
        hst = sb("hst", [P, HSTEPS, I])
        ysb = sb("ysb", [P, I])
        sg = sb("sg", [P, 2, MI, P])
        vg = sb("vg", [P, MI, P])
        r1 = sb("r1", [P, H])
        st1 = sb("st1", [P, 12])
        x1 = sb("x1", [P, H])
        x1b = sb("x1b", [P, RING, H])
        x1T = sb("x1T", [P, MH, P])
        hid = sb("hid", [P, 2, MF, P])
        zt = sb("zt", [P, MF, P])
        kr = sb("kr", [P, MF, P])
        kf = sb("kf", [P, MF, P])
        r2 = sb("r2", [P, H])
        st2 = sb("st2", [P, 12])
        ot = sb("ot", [P, 2, H])

        aT = [bank("aT0"), bank("aT1")]
        xb = [bank("xb0"), bank("xb1")]
        yacc = bank("yacc")
        G0, G1, G2 = bank("G0"), bank("G1"), bank("G2")
        xsP = G0[:, :].bitcast(bf16)

        m_in = sem("weights_loaded")
        m_xn = [sem("xn_loaded0"), sem("xn_loaded1")]
        m_xk = [sem(f"xk_loaded{i}") for i in range(RING)]
        m_out = [sem("out_stored0"), sem("out_stored1")]
        s_set = {e: sem(f"setup_{e}") for e in ("dve", "act", "pool")}
        s_aT, s_xb = sem("aT_ready"), sem("xb_ready")
        s_ah, s_h = sem("ah_ready"), sem("h_ready")
        s_c = sem("c_products")
        s_exp, s_yev, s_yT, s_v, s_yg = map(sem, ("exp_ready", "y_copied", "yT_ready", "v_ready", "yg_ready"))
        s_xT, s_xTe, s_xkT, s_xkTe = map(sem, ("xT_ready", "xT_copied", "xkT_ready", "xkT_copied"))
        s_hs, s_hse = sem("hs_ready"), sem("hs_copied")
        s_cc, s_u = sem("conv_steps"), sem("u_ready")
        s_gate, s_sg = sem("gate_ready"), sem("silu_gate_ready")
        s_xd, s_sq, s_red, s_ra, s_rs, s_l = map(sem, ("xd_ready", "xd_squared", "xd_reduced", "rms_ln", "rms_ready", "norms_applied"))
        s_rc = sem("reduce_chain")
        s_fs, s_fse, s_dtp, s_e1, s_sp, s_dt = map(sem, ("small_ready", "small_copied", "dtp_ready", "dt_exp", "softplus_ready", "dt_ready"))
        s_xm = sem("split_steps")
        s_xsT, s_xse = sem("xsT_ready"), sem("xsT_copied")
        s_o, s_r1, s_b1, s_n1a, s_n1, s_x1, s_x1b = map(sem, ("out_proj_ready", "r1_ready", "ln1_stats", "ln1_ln", "ln1_rstd", "x1_ready", "x1b_ready"))
        s_q1 = sem("ln1_chain")
        s_x1T, s_x1Te = sem("x1T_ready"), sem("x1T_copied")
        s_hm = sem("hidden_ready")
        s_hidA, s_hidB = sem("first_hidden_copied"), sem("second_hidden_copied")
        s_z, s_k, s_f, s_sin, s_cs, s_q, s_act = map(sem, ("turns_ready", "turns_rounded", "turns_reduced", "sine_ready", "sine_scaled", "q_ready", "act_ready"))
        s_w2, s_r2, s_b2, s_n2a, s_n2, s_ln2 = map(sem, ("ffn_ready", "r2_ready", "ln2_stats", "ln2_ln", "ln2_rstd", "ln2_ready"))
        s_q2 = sem("ln2_chain")
        s_passed = sem("passed")

        def prow(name, rows=P):
            a, b = POFF[name]
            return prm[0:rows, a:b]

        N_LOADS = 9
        DVE_SETUP = 29

        block = ctx.enter_context(nc.Block())

        @block.sync
        def _(sp_):
            for dst, src in ((win[:, :, :], w_in), (cst[:, :], consts), (prm[:, :], params), (wx[:, :, :], w_x),
                             (wdt[:, :], w_dt), (wo[:, :, :], w_out), (wf1[:, :, :], w1), (wf2[:, :, :], w2),
                             (b2_bc[:, :], b2)):
                sp_.dma_start(dst, src).then_inc(m_in, 16)
            for slot in range(2):
                sp_.sem_inc(m_out[slot], 1)

            def body(j):
                if j.on(4):
                    sp_.wait_ge(s_xT, j.count(2))
                    slot = j.slot(4, 2)
                    for i in range(4):
                        sp_.dma_start(xn[32 * i:32 * (i + 1), slot, :], x_t[bass.ds(j.tile(4), 1), i, :, :, :]
                                      .rearrange("n h b c -> (n h) b c")).then_inc(m_xn[slot], 16)
                if j.on(0):
                    sp_.wait_ge(s_r1, j.count(-RING))
                    slot = j.slot(0, RING)
                    for g in range(4):
                        sp_.dma_start(xk[32 * g:32 * (g + 1), slot, :], x_t[bass.ds(j.tile(0), 1), g, :, :, :]
                                      .rearrange("n h b c -> (n h) b c")).then_inc(m_xk[slot], 16)
                if j.on(-4):
                    sp_.wait_ge(s_ln2, j.count(-4))
                    slot = j.slot(-4, 2)
                    for g in range(4):
                        sp_.dma_start(out_t[bass.ds(j.tile(-4), 1), g, :, :, :].rearrange("n h b c -> (n h) b c"),
                                      ot[32 * g:32 * (g + 1), slot, :]).then_inc(m_out[slot], 16)
            iterations(sp_, body)
            for slot in range(2):
                sp_.wait_ge(m_out[slot], 16 * 4 * TILES // 2 + 1)

        @block.tensor
        def _(pe):
            pe.wait_ge(m_in, 16 * N_LOADS)
            pe.wait_ge(s_set["dve"], DVE_SETUP)

            def scan_operands(j, t):
                if t == 0:
                    pe.wait_ge(s_exp, j.count(0))
                pe.wait_ge(s_ah, j.count(-1, 2 * TS, 2 * (t - 1)))
                for k in range(MI):
                    last = T.transpose(aT[t % 2][:, P * k:P * (k + 1)], a1[:, j.slot(0, 2), k, t, :], ident)
                last.then_inc(s_aT, 1)
                if t == 0:
                    pe.wait_ge(s_xse, j.count(0, 2))
                pe.wait_ge(s_h, j.count(-1, 2 * TS, 2 * (t - 1)))
                g, h = t % 4, t // 4
                rows = slice(32 * g, 32 * g + 24)
                T.matmul(xb[t % 2][:, :], sel[rows, :], xsT[rows, j.slot(0, 2), h, :],
                         start=True, stop=True).then_inc(s_xb, 1)

            def c_products(j, k, h):
                pe.wait_ge(s_h, j.count(k - 1, 2 * TS, 2 * (4 * h + 4)))
                if h == 0:
                    pe.wait_ge(s_sg, j.count(k - 1))
                columns = cz[:, j.slot(k, RING), :, :].rearrange("p h c -> p (h c)")
                for g in range(4):
                    t = 4 * h + g
                    last = T.matmul(yacc[32 * g:32 * g + 32, :], columns[:, 32 * t:32 * (t + 1)], hst[:, t % HSTEPS, :],
                                    start=(h == 0), stop=(h == 3))
                last.then_inc(s_c, 1)

            def up(outp, w, col0, m0, m1, rhs):
                for m in range(m0, m1):
                    for k in range(MH):
                        last = T.matmul(outp[:, P * (m - m0):P * (m - m0 + 1)],
                                        w[:, k, col0 + P * m:col0 + P * (m + 1)], rhs[:, k, :],
                                        start=(k == 0), stop=(k == MH - 1))
                return last

            def ffn_down(j, k, blocks):
                for b in blocks:
                    last = T.matmul(G0[:, 0:H], kf[:, b, :], wf2[:, b, :], start=(b == 0), stop=(b == MF - 1))
                if blocks[-1] == MF - 1:
                    last.then_inc(s_w2, 1)

            def out_proj(j, blocks):
                for m in blocks:
                    last = T.matmul(G2[:, 0:H], vg[:, m, :], wo[:, m, :], start=(m == 0), stop=(m == MI - 1))
                if blocks[-1] == MI - 1:
                    last.then_inc(s_o, 1)

            def body(j):
                for t in range(TS):
                    if j.on(0):
                        scan_operands(j, t)
                    if t == 0 and j.on(-3):
                        up(G1[:, 2 * P:4 * P], wf1, 0, 6, 8, x1T).then_inc(s_hm, 1)
                    if t == 0 and j.on(-4):
                        pe.wait_ge(s_act, j.count(-4))
                        pe.wait_ge(s_xse, min_tile(j, 0, 2))
                        if j.reg is None:
                            pe.wait_ge(s_r2, j.count(-5))
                        ffn_down(j, -4, (0, 1))
                    if t == 1 and j.on(-4):
                        ffn_down(j, -4, (2, 3))
                    if t == 1 and j.on(-1):
                        c_products(j, -1, 3)
                    if t == 2 and j.on(-4):
                        ffn_down(j, -4, (4, 5))
                    if t == 3 and j.on(-4):
                        ffn_down(j, -4, (6, 7))
                    if t == 2 and j.on(4):
                        pe.wait_ge(s_hidB, j.count(-3))
                        pe.wait_ge(s_dt, j.count(1))
                        slot = j.slot(4, 2)
                        pe.wait_ge(m_xn[slot], j.uses(4, 2) * (16 * 4))
                        for k in range(MH):
                            last = T.transpose(G1[:, P * k:P * (k + 1)], xn[:, slot, P * k:P * (k + 1)], ident)
                        last.then_inc(s_xT, 1)
                    if t in (3, 4) and j.on(-1):
                        if t == 3:
                            pe.wait_ge(s_xkTe, j.count(-1))
                            pe.wait_ge(s_yev, j.count(-1))
                        m = 2 * (t - 3)
                        last = up(yacc[:, P * m:P * (m + 2)], win, I, m, m + 2, xkT)
                        if t == 4:
                            last.then_inc(s_gate, 1)
                    if t in (5, 6) and j.on(-2):
                        pe.wait_ge(s_yg, j.count(-2))
                        out_proj(j, (0, 1) if t == 5 else (2, 3))
                    if t == 6 and j.on(2):
                        pe.wait_ge(s_u, j.count(2))
                        pe.wait_ge(s_xTe, min_tile(j, 4, 1))
                        pe.wait_ge(s_hidB, j.count(-3))
                        for m in range(MI):
                            last = T.matmul(G1[:, 0:XW], u[:, j.slot(2, RING), m, :], wx[:, m, :],
                                            start=(m == 0), stop=(m == MI - 1))
                        last.then_inc(s_xd, 1)
                    if t == 7 and j.on(0):
                        c_products(j, 0, 0)
                    if t in (8, 9) and j.on(4):
                        if t == 8:
                            pe.wait_ge(s_xTe, j.count(4))
                            pe.wait_ge(s_r2, j.count(-4))
                            pe.wait_ge(s_hse, j.count(3))
                            pe.wait_ge(s_xse, j.count(0, 2))
                        m = 2 * (t - 8)
                        last = up(G0[:, P * m:P * (m + 2)], win, 0, m, m + 2, xT)
                        if t == 9:
                            last.then_inc(s_hs, 1)
                    if t == 9 and j.on(0):
                        pe.wait_ge(s_r1, j.count(-2))
                        slot = j.slot(0, RING)
                        pe.wait_ge(m_xk[slot], j.uses(0, RING) * (16 * 4))
                        for k in range(MH):
                            last = T.transpose(G2[:, P * k:P * (k + 1)], xk[:, slot, P * k:P * (k + 1)], ident)
                        last.then_inc(s_xkT, 1)
                    if t == 10 and j.on(0):
                        c_products(j, 0, 1)
                    if t == 10 and j.on(2):
                        pe.wait_ge(s_l, j.count(2))
                        T.transpose(G1[:, 256:384], lc[:, :], ident)
                        T.transpose(G1[0:R, 128:256], dtn[:, :], ident)
                        T.matmul(G1[:, 384:384 + TS], lb[:, :], steps_of, start=True, stop=True).then_inc(s_fs, 1)
                    if t == 11 and j.on(-2):
                        pe.wait_ge(s_x1, j.count(-2))
                        pe.wait_ge(s_xkTe, min_tile(j, 0, 1))
                        for k in range(MH):
                            last = T.transpose(G2[:, P * k:P * (k + 1)], x1[:, P * k:P * (k + 1)], ident)
                        last.then_inc(s_x1T, 1)
                    if t in (11, 13) and j.on(1):
                        part = (t - 11) // 2
                        if part == 0:
                            pe.wait_ge(s_xm, j.count(1, SPLITS))
                            pe.wait_ge(s_hse, min_tile(j, 4, 1))
                            pe.wait_ge(s_r2, j.count(-4))
                        else:
                            pe.wait_ge(s_xse, j.count(0, 2, 1))
                        for h in (2 * part, 2 * part + 1):
                            for m in range(MI):
                                c = I * (h - 2 * part) + P * m
                                last = T.transpose(xsP[:, c:c + P],
                                                   xs[:, m, 4 * h:4 * h + 4, :, :].rearrange("p g a b -> p (g a b)"), identb[:, :])
                        last.then_inc(s_xsT, 1)
                    if t == 12 and j.on(2):
                        pe.wait_ge(s_fse, j.count(2))
                        for m in range(MI):
                            last = T.matmul(G1[:, P * m:P * (m + 1)], wdt[:, P * m:P * (m + 1)], dtT[:, :],
                                            start=True, stop=True)
                        last.then_inc(s_dtp, 1)
                    if t in (12, 13) and j.on(-2):
                        pe.wait_ge(s_x1Te, j.count(-2))
                        m = 2 * (t - 12)
                        last = up(G2[:, P * m:P * (m + 2)], wf1, 0, m, m + 2, x1T)
                        if t == 13:
                            last.then_inc(s_hm, 1)
                    if t == 14 and j.on(0):
                        c_products(j, 0, 2)
                    if t == 15 and j.on(-2):
                        pe.wait_ge(s_dt, min_tile(j, 2, 1))
                        pe.wait_ge(s_hidB, j.count(-3))
                        up(G1[:, 0:2 * P], wf1, 0, 4, 6, x1T)
                    if t == 15 and j.on(-1):
                        pe.wait_ge(s_yev, j.count(-1))
                        pe.wait_ge(s_hidA, j.count(-2))
                        pe.wait_ge(s_xkTe, min_tile(j, 0, 1))
                        for m in range(MI):
                            last = T.transpose(G2[:, P * m:P * (m + 1)], ysb[:, P * m:P * (m + 1)], unperm)
                        last.then_inc(s_yT, 1)
            iterations(pe, body)

        @block.scalar
        def _(act):
            act.wait_ge(m_in, 16 * N_LOADS)
            act.wait_ge(s_set["dve"], DVE_SETUP - 5)

            def exp_ln_tables():
                S.add_instruction(mybir.InstLoadActFuncSet(name=nc.get_next_instruction_name(), act_func_set_id=EXP_LN_SET,
                                                           engine=mybir.EngineType.Activation))

            S.activation(tt[:, 3, :], tt[:, 1, :], ACT.Sin, scale=SIN_SCALE).then_inc(s_set["act"], 1)
            S.activation(tt[:, 4, :], tt[:, 2, :], ACT.Sin, scale=SIN_SCALE).then_inc(s_set["act"], 1)
            S.activation(Aneg[:, :], prow("A_log"), ACT.Exp).then_inc(s_set["act"], 1)
            exp_ln_tables()
            act.wait_ge(s_set["dve"], DVE_SETUP)

            def flat(ap):
                return ap.rearrange("p a b -> p (a b)")

            def exponentials(j, e0, e1):
                if e0 == 0:
                    act.wait_ge(s_dt, j.count(1))
                    act.wait_ge(s_aT, j.count(-1, TS))
                for e in range(e0, e1):
                    m, n = divmod(e, N)
                    o = a1[:, j.slot(1, 2), m, :, n:P:N]
                    i = dts[:, j.slot(1, 2), m, :].rearrange("p (t b) -> p t b", b=B)
                    last = S.activation(o, i, ACT.Exp, scale=Aneg[:, e:e + 1])
                if e1 == MI * N:
                    last.then_inc(s_exp, 1)

            def rstd(src, dst, eps, s_half, s_done, need):
                S.activation(dst, src, ACT.Ln, bias=eps).then_inc(s_half, 1)
                act.wait_ge(s_half, need)
                S.activation(dst, dst, ACT.Exp, scale=-0.5).then_inc(s_done, 1)

            def body(j):
                for t in range(TS):
                    if j.on(1) and EXPS[t + 1] > EXPS[t]:
                        exponentials(j, EXPS[t], EXPS[t + 1])
                    if t == 1 and j.on(-3):
                        hidden_copy(j, -3)
                    if t == 2 and j.on(-1):
                        act.wait_ge(s_c, j.count(-1, 4))
                        act.wait_ge(s_yT, j.count(-2))
                        S.copy(ysb[:, :], yacc[:, :]).then_inc(s_yev, 1)
                    if t == 3 and j.on(4):
                        act.wait_ge(s_xT, j.count(4))
                        act.wait_ge(s_hs, j.count(3))
                        S.copy(flat(xT[:, :, :]), G1[:, 0:H]).then_inc(s_xTe, 1)
                    if t == 10 and j.on(0):
                        act.wait_ge(s_xkT, j.count(0))
                        act.wait_ge(s_gate, j.count(-1))
                        S.copy(flat(xkT[:, :, :]), G2[:, 0:H]).then_inc(s_xkTe, 1)
                    if t == 4 and j.on(2):
                        act.wait_ge(s_cc, j.count(2, CONVS))
                        act.wait_ge(s_v, j.count(-2))
                        S.activation(u[:, j.slot(2, RING), :, :], cv[:, 0, :, :], ACT.Silu).then_inc(s_u, 1)
                    if t == 4 and j.on(-3):
                        act.wait_ge(s_f, j.count(-3))
                        act.wait_ge(s_w2, j.count(-4))
                        S.activation(kf[:, :, :], zt[:, :, :], ACT.Sin, scale=SIN_SCALE).then_inc(s_sin, 1)
                    if t == 4 and j.on(-1):
                        act.wait_ge(s_gate, j.count(-1))
                        act.wait_ge(s_yg, j.count(-3))
                        S.activation(flat(sg[:, j.slot(-1, 2), :, :]), yacc[:, :], ACT.Silu).then_inc(s_sg, 1)
                    if t == 4:
                        exp_ln_tables()
                    if t == 5 and j.on(-4):
                        act.wait_ge(s_b2, j.count(-4))
                        rstd(st2[:, 7:8], st2[:, 8:9], eps_ln[:, :], s_n2a, s_n2, j.count(-4))
                    if t == 6 and j.on(2):
                        act.wait_ge(s_xd, j.count(2))
                        act.wait_ge(s_red, j.count(1))
                        S.activation(xd2[:, :], G1[:, 0:XW], ACT.Square).then_inc(s_sq, 1)
                    if t == 8 and j.on(2):
                        act.wait_ge(s_red, j.count(2))
                        rstd(ms[:, 4:7], rs[:, 0:3], eps_rms[:, :], s_ra, s_rs, j.count(2))
                    if t == 8 and j.on(-2):
                        act.wait_ge(s_b1, j.count(-2))
                        rstd(st1[:, 7:8], st1[:, 8:9], eps_ln[:, :], s_n1a, s_n1, j.count(-2))
                    if t == 10 and j.on(4):
                        hs_copy(j)
                    if t == 11 and j.on(-2):
                        act.wait_ge(s_x1T, j.count(-2))
                        act.wait_ge(s_hm, j.count(-3, 2))
                        S.copy(flat(x1T[:, :, :]), G2[:, 0:H]).then_inc(s_x1Te, 1)
                    if t == 13 and j.on(2):
                        act.wait_ge(s_dtp, j.count(2))
                        act.wait_ge(s_dt, j.count(1))
                        S.activation(flat(sp[:, :, :]), G1[:, :], ACT.Exp).then_inc(s_e1, 1)
                        act.wait_ge(s_e1, j.count(2))
                        S.activation(flat(sp[:, :, :]), flat(sp[:, :, :]), ACT.Ln, bias=one[:, :]).then_inc(s_sp, 1)
                    if t in (12, 14) and j.on(1):
                        part = (t - 12) // 2
                        act.wait_ge(s_xsT, j.count(0, 2, part + 1))
                        act.wait_ge(s_xb, j.count(-1, TS))
                        S.copy(flat(xsT[:, j.slot(1, 2), 2 * part:2 * part + 2, :]), xsP).then_inc(s_xse, 1)

            def hidden_copy(j, k):
                act.wait_ge(s_hm, j.count(k, 2))
                for m in range(4, MF):
                    last = S.activation(hid[:, j.slot(k, 2), m, :], G1[:, P * (m - 4):P * (m - 3)], ACT.Identity,
                                        bias=prow("b1")[:, m:m + 1])
                last.then_inc(s_hidB, 1)

            def hs_copy(j):
                act.wait_ge(s_hs, j.count(4))
                act.wait_ge(s_cc, j.count(1, CONVS))
                slot = j.slot(4, RING)
                src = G0[:, :].rearrange("p (m t) -> p m t", m=MI)
                last = S.copy(hs[:, :, B + P * slot:B + P * (slot + 1)], src)
                if slot == RING - 1:
                    last = S.copy(hs[:, :, 0:B], src[:, :, P - B:P])
                if slot == 0:
                    last = S.copy(hs[:, :, B + RT:B + RT + 2 * B], src[:, :, 0:2 * B])
                last.then_inc(s_hse, 1)

            iterations(act, body)

        @block.vector
        def _(dve):
            dve.wait_ge(m_in, 16 * N_LOADS)
            done = [0]

            def setup(ins):
                ins.then_inc(s_set["dve"], 1)
                done[0] += 1
                dve.wait_ge(s_set["dve"], done[0])

            th, inv = prow("theta"), INV_2PI
            setup(V.tensor_scalar(tt[:, 0, :], th, inv, ROUND, MUL, ADD))
            setup(V.tensor_scalar(tt[:, 0, :], tt[:, 0, :], ROUND, None, SUB))
            setup(V.scalar_tensor_tensor(tt[:, 5, :], tt[:, 0, :], -PI_A, th, MUL, ADD))
            setup(V.scalar_tensor_tensor(tt[:, 5, :], tt[:, 0, :], -PI_B, tt[:, 5, :], MUL, ADD))
            setup(V.scalar_tensor_tensor(tt[:, 5, :], tt[:, 0, :], -PI_C, tt[:, 5, :], MUL, ADD))
            setup(V.tensor_scalar(turn0[:, :], tt[:, 5, :], inv, None, MUL))
            setup(V.tensor_scalar(tt[:, 1, :], turn0[:, :], 0.5, -0.5, MIN, MAX))
            setup(V.tensor_scalar(tt[:, 6, :], turn0[:, :], 0.25, None, ADD))
            setup(V.tensor_scalar(tt[:, 7, :], tt[:, 6, :], ROUND, ROUND, ADD, SUB))
            setup(V.tensor_tensor(tt[:, 2, :], tt[:, 6, :], tt[:, 7, :], SUB))
            setup(V.memset(eps_rms[:, :], EPS_RMS))
            setup(V.memset(eps_ln[:, :], EPS_LN))
            setup(V.memset(one[:, :], 1.0))
            setup(V.tensor_copy(identb[:, :], ident))
            setup(V.tensor_copy(sel[:, :], cst[:, 2 * P:3 * P]))
            setup(V.tensor_scalar(wx[:, :, 0:R], wx[:, :, 0:R], R ** -0.5, None, MUL))
            setup(V.tensor_scalar(wx[:, :, R:XW], wx[:, :, R:XW], N ** -0.5, None, MUL))
            setup(V.tensor_scalar(prow("bw"), prow("bw"), N ** 0.5, None, MUL))
            setup(V.tensor_scalar(prow("cw"), prow("cw"), N ** 0.5, None, MUL))
            setup(V.tensor_scalar(wdt[0:R, :], wdt[0:R, :], prow("dtw", R), R ** 0.5, MUL, MUL))
            setup(V.memset(dtT[R:R + 1, :], 1.0))
            setup(V.memset(cz[:, :, :, :], 0.0))
            setup(V.memset(xs[:, :, :, :, :], 0.0))
            setup(V.memset(hst[:, HSTEPS - 1, :], 0.0))
            dve.wait_ge(s_set["act"], 3)
            setup(V.tensor_scalar(Aneg[:, :], Aneg[:, :], -1.0, None, MUL))
            setup(V.tensor_tensor(tt[:, 4, :], tt[:, 4, :], prow("w_re"), MUL))
            setup(V.tensor_tensor(tt[:, 3, :], tt[:, 3, :], prow("w_im"), MUL))
            setup(V.tensor_tensor(tt[:, 4, :], tt[:, 4, :], tt[:, 3, :], ADD))
            setup(V.scalar_tensor_tensor(amp[:, :], tt[:, 4, :], 0.1, prow("w_im"), MUL, MUL))
            assert done[0] == DVE_SETUP

            def scan_step(j, t, between):
                halves = [slice(0, I)] if t in WHOLE else [slice(0, I // 2), slice(I // 2, I)]
                n = 2 // len(halves)
                dve.wait_ge(s_aT, j.count(-1, TS, t + 1))
                for i, c in enumerate(halves):
                    dve.wait_ge(s_h, j.count(-1, 2 * TS, 2 * t - 2 + n * (i + 1)))
                    V.tensor_tensor(ah[:, c], aT[t % 2][:, c], hst[:, (t - 1) % HSTEPS, c], MUL).then_inc(s_ah, n)
                between(j, t)
                dve.wait_ge(s_xb, j.count(-1, TS, t + 1))
                if t % 4 == 0:
                    dve.wait_ge(s_c, j.count(-1, 4, t // 4 - 1))
                for i, c in enumerate(halves):
                    dve.wait_ge(s_ah, j.count(-1, 2 * TS, 2 * t + n * (i + 1)))
                    V.scalar_tensor_tensor(hst[:, t % HSTEPS, c], xb[t % 2][:, c], bs[:, j.slot(0, RING), t:t + 1], ah[:, c],
                                           MUL, ADD).then_inc(s_h, n)

            v3 = lambda ap: ap.rearrange("p (b n) -> p b n", n=N)

            def mid(j, t):
                if t == 1 and j.on(-2):
                    dve.wait_ge(s_yT, j.count(-2))
                    dve.wait_ge(s_o, j.count(-3))
                    y_plus_uD(j, (0, 1))
                if t == 2 and j.on(-3):
                    dve.wait_ge(s_z, j.count(-3, 2))
                    dve.wait_ge(s_f, j.count(-4))
                    V.tensor_scalar(kr[:, 0:MF // 2, :], zt[:, 0:MF // 2, :], ROUND, ROUND, ADD, SUB)
                if t == 4 and j.on(-4):
                    dve.wait_ge(s_w2, j.count(-4))
                    dve.wait_ge(s_x1b, j.count(-4))
                    V.tensor_tensor(r2[:, :], G0[:, 0:H], x1b[:, j.slot(-4, RING), :], ADD).then_inc(s_r2, 1)
                if t == 7 and j.on(2):
                    dve.wait_ge(s_sq, j.count(2))
                    dve.wait_ge(s_rs, j.count(1))
                    V.tensor_reduce(ms[:, 0:6], xd2[:, :].rearrange("p (a b) -> p a b", b=N), AX.X, ADD).then_inc(s_rc, 1)
                if t == 10 and j.on(2):
                    dve.wait_ge(s_fs, j.count(2))
                    dve.wait_ge(s_dtp, j.count(1))
                    V.tensor_copy(dtT[0:R, :], G1[0:R, 128:256])
                    V.tensor_scalar(bs[:, j.slot(2, RING), :], G1[:, 384:384 + TS], prow("bw"), None, MUL)
                if t == 8 and j.on(-4):
                    dve.wait_ge(s_n2, j.count(-4))
                    slot = j.slot(-4, 2)
                    dve.wait_ge(m_out[slot], (j.uses(-4, 2) - 1) * (16 * 4) + 1)
                    V.tensor_scalar(ot[:, slot, :], r2[:, :], st2[:, 6:7], st2[:, 8:9], SUB, MUL).then_inc(s_ln2, 1)
                if t == 13 and j.on(-3):
                    dve.wait_ge(s_q, j.count(-3))
                    V.tensor_scalar(kf[:, 0:MF // 2, :], kf[:, 0:MF // 2, :], 0.0, None, MAX)
                if t == 14 and j.on(2):
                    dve.wait_ge(s_sp, j.count(2))
                    dve.wait_ge(s_exp, j.count(0))
                    dve.wait_ge(s_xm, j.count(0, SPLITS))
                    V.scalar_tensor_tensor(dts[:, j.slot(2, 2), :, :].rearrange("p a b -> p (a b)"), G1[:, :], SP_CAP,
                                           sp[:, :, :].rearrange("p a b -> p (a b)"), MAX, MIN).then_inc(s_dt, 1)

            def post(j, t):
                if t == 1 and j.on(-2):
                    y_plus_uD(j, (2, 3))
                if t == 2 and j.on(-3):
                    V.tensor_scalar(kr[:, MF // 2:, :], zt[:, MF // 2:, :], ROUND, ROUND, ADD, SUB).then_inc(s_k, 1)
                if t == 4 and j.on(-4):
                    dve.wait_ge(s_r2, j.count(-4))
                    V.bn_stats(st2[:, 0:6], r2[:, :]).then_inc(s_q2, 1)
                    moments(st2, s_q2, s_b2, j.count(-4))
                if t == 7 and j.on(2):
                    dve.wait_ge(s_rc, j.count(2))
                    V.tensor_reduce(ms[:, 6:7], ms[:, 0:4], AX.X, ADD).then_inc(s_red, 1)
                if t == 7 and j.on(-2):
                    dve.wait_ge(s_o, j.count(-2))
                    dve.wait_ge(s_x1, j.count(-3))
                    V.tensor_tensor(r1[:, :], G2[:, 0:H], xk[:, j.slot(-2, RING), :], ADD).then_inc(s_r1, 1)
                    dve.wait_ge(s_r1, j.count(-2))
                    V.bn_stats(st1[:, 0:6], r1[:, :]).then_inc(s_q1, 1)
                    moments(st1, s_q1, s_b1, j.count(-2))
                if t == 8 and j.on(2):
                    dve.wait_ge(s_rs, j.count(2))
                    dve.wait_ge(s_fs, j.count(1))
                    V.tensor_scalar(dtn[:, :], G1[:, 0:R], rs[:, 2:3], None, MUL)
                    for dst, c0, q in ((lb, R, 0), (lc, R + N, 1)):
                        src = G1[:, c0:c0 + N].rearrange("p (a n) -> p a n", a=1).to_broadcast([P, B, N])
                        last = V.scalar_tensor_tensor(v3(dst[:, :]), src, rs[:, q:q + 1], v3(mask), MUL, MUL)
                    last.then_inc(s_l, 1)
                if t == 9 and j.on(-2):
                    dve.wait_ge(s_n1, j.count(-2))
                    dve.wait_ge(s_x1T, j.count(-3))
                    dve.wait_ge(s_x1b, j.count(-3))
                    V.tensor_scalar(x1[:, :], r1[:, :], st1[:, 6:7], st1[:, 8:9], SUB, MUL).then_inc(s_x1, 1)
                if t == 10 and j.on(2):
                    dve.wait_ge(s_c, j.count(-2, 4))
                    V.tensor_scalar(cz[:, j.slot(2, RING), :, 0:P].rearrange("p h (g c) -> p h g c", g=4)[:, :, :, 0:B],
                                    G1[:, 256:384].rearrange("p (h g b) -> p h g b", h=4, g=4),
                                    prow("cw"), None, MUL).then_inc(s_fse, 1)
                if t == 13 and j.on(-3):
                    V.tensor_scalar(kf[:, MF // 2:, :], kf[:, MF // 2:, :], 0.0, None, MAX).then_inc(s_act, 1)
                if t == 14 and j.on(-2):
                    dve.wait_ge(s_hm, j.count(-3, 2, 1))
                    dve.wait_ge(s_q, j.count(-4))
                    hidden_copy(j, (0, 1, 2, 3))
                if t == 10 and j.on(-4):
                    dve.wait_ge(s_ln2, j.count(-4))

            def y_plus_uD(j, blocks):
                for m in blocks:
                    last = V.scalar_tensor_tensor(vg[:, m, :], u[:, j.slot(-2, RING), m, :], prow("D")[:, m:m + 1],
                                                  G2[:, P * m:P * (m + 1)], MUL, ADD)
                if blocks[-1] == MI - 1:
                    last.then_inc(s_v, 1)

            def hidden_copy(j, blocks):
                for m in blocks:
                    last = V.tensor_scalar(hid[:, j.slot(-2, 2), m, :], G2[:, P * m:P * (m + 1)],
                                           prow("b1")[:, m:m + 1], None, ADD)
                if blocks[-1] == 3:
                    last.then_inc(s_hidA, 1)

            def moments(st, s_chain, s_done, need):
                dve.wait_ge(s_chain, need)
                dve.sem_inc(s_passed, 1)
                V.bn_aggr(st[:, 6:8], st[:, 0:6]).then_inc(s_done, 1)

            def body(j):
                for t in range(TS):
                    if j.on(0):
                        scan_step(j, t, mid)
                    else:
                        mid(j, t)
                    post(j, t)
            iterations(dve, body)

        @block.gpsimd
        def _(pool):
            pool.wait_ge(m_in, 16 * N_LOADS)
            pool.wait_ge(s_set["dve"], DVE_SETUP)
            G.memset(hs[:, :, 0:B], 0.0).then_inc(s_set["pool"], 1)
            pool.wait_ge(s_set["pool"], 1)

            def alone():
                pool.sem_inc(s_passed, 1)

            def turns(j, k, half):
                pool.wait_ge((s_hidA, s_hidB)[half], j.count(k))
                if half == 0:
                    pool.wait_ge(s_sin, j.count(k - 1))
                alone()
                for m in range(4 * half, 4 * half + 4):
                    last = G.tensor_scalar(zt[:, m, :], hid[:, j.slot(k, 2), m, :], 0.1 * INV_2PI, turn0[:, m:m + 1], MUL, ADD)
                last.then_inc(s_z, 1)

            def body(j):
                flat = lambda ap: ap.rearrange("p a b -> p (a b)")
                if j.on(-3):
                    turns(j, -3, 1)
                if j.on(-2):
                    pool.wait_ge(s_v, j.count(-2))
                    pool.wait_ge(s_sg, j.count(-2))
                    G.tensor_tensor(flat(vg[:, :, :]), flat(vg[:, :, :]), flat(sg[:, j.slot(-2, 2), :, :]), MUL).then_inc(s_yg, 1)
                if j.on(-3):
                    pool.wait_ge(s_z, j.count(-3, 2))
                    pool.wait_ge(s_k, j.count(-3))
                    G.tensor_tensor(flat(zt[:, :, :]), flat(zt[:, :, :]), flat(kr[:, :, :]), SUB).then_inc(s_f, 1)
                if j.on(1):
                    pool.wait_ge(s_dt, j.count(1))
                    pool.wait_ge(s_u, j.count(1))
                    pool.wait_ge(s_xsT, j.count(0, 2))
                    base = lambda i: j.count(0, SPLITS, i)
                    part = lambda a: xs[:, :, :, a, :].rearrange("p m t b -> p (m t) b")
                    v = lambda ap: ap.rearrange("p m (t b) -> p (m t) b", b=B)
                    x0, x1_ = xf[:, 0, :, :], xf[:, 1, :, :]
                    G.tensor_tensor(flat(x0), flat(dts[:, j.slot(1, 2), :, :]), flat(u[:, j.slot(1, RING), :, :]), MUL).then_inc(s_xm, 1)
                    pool.wait_ge(s_xm, base(1))
                    alone()
                    G.tensor_scalar(part(0), v(x0), 1.0, 1.0, MUL, MUL).then_inc(s_xm, 1)
                    pool.wait_ge(s_xm, base(2))
                    G.tensor_tensor(v(x1_), v(x0), part(0), SUB).then_inc(s_xm, 1)
                    pool.wait_ge(s_xm, base(3))
                    alone()
                    G.tensor_scalar(part(1), v(x1_), 1.0, 1.0, MUL, MUL).then_inc(s_xm, 1)
                    pool.wait_ge(s_xm, base(4))
                    G.tensor_tensor(part(2), v(x1_), part(1), SUB).then_inc(s_xm, 1)
                if j.on(-3):
                    pool.wait_ge(s_sin, j.count(-3))
                    alone()
                    for m in range(MF):
                        last = G.tensor_scalar(kf[:, m, :], kf[:, m, :], amp[:, m:m + 1], 1.0, MUL, MUL)
                    last.then_inc(s_cs, 1)
                    pool.wait_ge(s_cs, j.count(-3))
                    G.tensor_tensor(flat(kf[:, :, :]), flat(kf[:, :, :]), flat(hid[:, j.slot(-3, 2), :, :]), ADD).then_inc(s_q, 1)
                if j.on(-2):
                    pool.wait_ge(s_x1, j.count(-2))
                    G.tensor_tensor(x1b[:, j.slot(-2, RING), :], x1[:, :], b2_bc[:, :], ADD).then_inc(s_x1b, 1)
                if j.on(3):
                    if j.on(4):
                        pool.wait_ge(s_hse, j.count(4))
                    else:
                        pool.wait_ge(s_hse, j.count(3))
                        G.memset(hs[:, :, B + RT:B + RT + 2 * B], 0.0).then_inc(s_set["pool"], 1)
                        pool.wait_ge(s_set["pool"], 2)
                    pool.wait_ge(s_u, j.count(2))
                    alone()
                    base = lambda i: j.count(2, CONVS, i)
                    c0 = P * j.slot(3, RING)
                    for k in range(K):
                        for m in range(MI):
                            src = hs[:, m, c0 + B * k:c0 + B * k + P]
                            w = prow("conv_w")[:, K * m + k:K * m + k + 1]
                            if k == 0:
                                last = G.tensor_scalar(cv[:, k, m, :], src, w, prow("conv_b")[:, m:m + 1], MUL, ADD)
                            else:
                                last = G.tensor_scalar(cv[:, k, m, :], src, w, 1.0, MUL, MUL)
                    last.then_inc(s_cc, 1)
                    pool.wait_ge(s_cc, base(1))
                    G.tensor_tensor(flat(cv[:, 0, :, :]), flat(cv[:, 0, :, :]), flat(cv[:, 1, :, :]), ADD)
                    G.tensor_tensor(flat(cv[:, 2, :, :]), flat(cv[:, 2, :, :]), flat(cv[:, 3, :, :]), ADD).then_inc(s_cc, 1)
                    pool.wait_ge(s_cc, base(2))
                    G.tensor_tensor(flat(cv[:, 0, :, :]), flat(cv[:, 0, :, :]), flat(cv[:, 2, :, :]), ADD).then_inc(s_cc, 1)
                if j.on(-2):
                    turns(j, -2, 0)
            iterations(pool, body)


def kernel(**inputs):
    import numpy as np
    import concourse.bacc as bacc
    from concourse.bass_utils import run_bass_kernel_spmd

    a = {k[3:]: np.asarray(v) for k, v in inputs.items()}

    def cols(v, n):
        return np.ascontiguousarray(np.moveaxis(v.reshape(n, P, -1), 0, 1)).reshape(P, -1)

    rows = {"conv_w": cols(a["attn_conv_w"], MI), "conv_b": cols(a["attn_conv_b"], MI), "A_log": cols(a["attn_A_log"], MI),
            "D": cols(a["attn_D"], MI), "b1": cols(a["ffn_b1"], MF), "theta": cols(a["ffn_quantum_phases"], MF),
            "w_re": cols(a["ffn_quantum_weights_real"], MF), "w_im": cols(a["ffn_quantum_weights_imag"], MF),
            "bw": np.tile(a["attn_b_ln_w"], B)[:, None], "cw": np.tile(a["attn_c_ln_w"], B)[:, None],
            "dtw": np.tile(a["attn_dt_ln_w"], P // R)[:, None]}
    params = np.concatenate([rows[k] for k in PCOLS], axis=1)

    p = np.arange(P)
    ident = np.eye(P, dtype=np.float32)
    mask = (p[:, None] % B == p[None, :] // N).astype(np.float32)
    sel = mask * (p[:, None] % 32 < 24)
    unperm = (p[:, None] // 32 + 4 * (p[:, None] % 32 // B) == p[None, :] // B) * (p[:, None] % B == p[None, :] % B)
    steps = p[:, None] // B == np.arange(TS)[None, :]
    consts = np.concatenate([ident, mask, sel, unperm, steps], axis=1).astype(np.float32)

    def blocks(v, n):
        return np.ascontiguousarray(v.reshape(n, P, -1).transpose(1, 0, 2))

    arrays = {
        "x": a["attn_hidden_states"],
        "w_in": blocks(a["attn_in_proj_w"].T, MH), "w_x": blocks(a["attn_x_proj_w"].T, MI),
        "w_dt": np.concatenate([a["attn_dt_proj_w"].T, a["attn_dt_proj_b"][None, :]], axis=0),
        "w_out": blocks(a["attn_out_proj_w"].T, MI), "w1": blocks(a["ffn_W1"], MH), "w2": blocks(a["ffn_W2"], MF),
        "params": params, "b2": np.ascontiguousarray(np.broadcast_to(a["ffn_b2"], (P, H))), "consts": consts,
    }
    nc = bacc.Bacc("TRN2", target_bir_lowering=False, num_devices=1, dynamic_dma_scratch_size=1024)
    feeds, args = {}, []
    for name, v in arrays.items():
        v = np.ascontiguousarray(v)
        feeds[f"in_{name}"] = v
        args.append(nc.dram_tensor(f"in_{name}", v.shape, mybir.dt.from_np(v.dtype), kind="ExternalInput").ap())
    args.append(nc.dram_tensor("out_0", (B, L, H), mybir.dt.float32, kind="ExternalOutput").ap())
    mamba_ffn_kernel(nc, *args)
    r = run_bass_kernel_spmd(nc, [feeds], core_ids=[0])
    return r.results[0]["out_0"]
```
